# Optimizing a Trainium2 kernel written in Bass

```python
import numpy as np
import jax
import jax.numpy as jnp

def _softmax(x, axis=-1):
    return jax.nn.softmax(x, axis=axis)

def _gelu(x):
    return jax.nn.gelu(x, approximate=True)

def _silu(x):
    return jax.nn.silu(x)

def _sigmoid(x):
    return jax.nn.sigmoid(x)

def _layernorm(x, axis=-1, eps=1e-05):
    m = jnp.mean(x, axis=axis, keepdims=True)
    v = jnp.var(x, axis=axis, keepdims=True)
    return (x - m) / jnp.sqrt(v + eps)

def _scatter_add(tgt, idx, src, axis=0):
    return tgt.at[idx].add(src)

def _segment_sum(src, seg, n):
    return jax.ops.segment_sum(src, seg, n)
kernel_name = 'mk_flamingo_gated_d2_seqx_r8_fec106'

def setup_inputs(seed: int=0):
    np.random.seed(seed)
    _w = jnp.asarray

    def _rec_inputs():
        import jax
        import jax.numpy as jnp
        _rk = jax.random.key(seed)
        x = 0.5 + 0.2887 * jax.random.normal(jax.random.fold_in(_rk, 1), (4, 256, 256), jnp.float32)
        _lenS = 256 - jax.random.randint(jax.random.fold_in(_rk, 7), (4,), 0, max(1, 256 // 4) + 1, jnp.int32)
        _lenS2 = 256 - jax.random.randint(jax.random.fold_in(_rk, 8), (4,), 0, max(1, 256 // 4) + 1, jnp.int32)
        _ctx_512P = jax.random.normal(jax.random.fold_in(_rk, 11), (4, 16, 64), jnp.float32)
        _ctx_512c = jax.random.dirichlet(jax.random.fold_in(_rk, 511), 0.3 * jnp.ones((16,), jnp.float32), (4, 256))
        _ctx_512t = jnp.einsum('bsk,bkd->bsd', _ctx_512c, _ctx_512P)
        _ctx_512t = _ctx_512t * jax.lax.rsqrt(jnp.mean(jnp.square(_ctx_512t)) + 1e-12) * 0.953939
        ctx_512 = -0.000392918 + 0.999932 * (_ctx_512t + 0.3 * jax.random.normal(jax.random.fold_in(_rk, 611), (4, 256, 64), jnp.float32))
        _validS = jnp.arange(256)[None, :] < _lenS[:, None]
        _validS2 = jnp.arange(256)[None, :] < _lenS2[:, None]
        _causal = jnp.tril(jnp.ones((256, 256), dtype=bool))
        mask_SxS2_bk1 = jnp.broadcast_to(_validS2[0:1, :], (256, 256))
        mask_BxS2_bf0 = jnp.logical_not(jnp.ones((4, 256), dtype=bool))
        _g = jax.random.normal(jax.random.fold_in(_rk, 9001), (2, 2), jnp.float32)
        _g = jnp.sign(_g) * jnp.maximum(jnp.abs(_g), 1.0) + (_g == 0) * 1.0
        g_xattn = _g[0]
        g_ffn = _g[1]
        return (x, ctx_512, mask_SxS2_bk1, mask_BxS2_bf0, g_xattn, g_ffn)
    x, ctx_512, mask_SxS2_bk1, mask_BxS2_bf0, g_xattn, g_ffn = _rec_inputs()

    def _L0_xattn_setup():
        import jax, jax.numpy as jnp
        import numpy as np
        B, N, D = (16, 256, 64)
        H = 4
        TOP_K_RATIO = 0.3
        key = jax.random.key(seed)
        k1, k2, k3, k4 = jax.random.split(key, 4)
        h = jax.random.normal(k1, (B, N, D), dtype=jnp.float32)
        adj_raw = jax.random.uniform(k2, (B, N, N), dtype=jnp.float32)
        lim = 1.0 / np.sqrt(D)
        Wq = jax.random.uniform(k3, (D, D), minval=-lim, maxval=lim, dtype=jnp.float32)
        Wk = jax.random.uniform(k4, (D, D), minval=-lim, maxval=lim, dtype=jnp.float32)
        gamma_raw = jnp.float32(-0.85)
        return {'h': h, 'adj_raw': adj_raw, 'Wq': Wq, 'Wk': Wk, 'gamma_raw': gamma_raw}
    _L0_xattn_all = _L0_xattn_setup()
    _L0_xattn_in = {k: v for k, v in _L0_xattn_all.items() if k in ('Wq', 'Wk', 'gamma_raw')}
    del _L0_xattn_all

    def _L0_ffn_setup():
        import jax, jax.numpy as jnp
        import numpy as np
        NUM_EXPERTS = 4
        key = jax.random.key(seed)
        k1, k2, k3 = jax.random.split(key, 3)
        B, N, H = (8, 256, 256)
        E = NUM_EXPERTS
        I = H * 4 // E
        x = jax.random.normal(k1, (B, N, H), dtype=jnp.float32)
        gate_up_proj = jax.random.normal(k2, (E, H, 2 * I), dtype=jnp.float32) * 0.02
        down_proj = jax.random.normal(k3, (E, I, H), dtype=jnp.float32) * 0.02
        return {'x': x, 'gate_up_proj': gate_up_proj, 'down_proj': down_proj}
    _L0_ffn_all = _L0_ffn_setup()
    _L0_ffn_in = {k: v for k, v in _L0_ffn_all.items() if k in ('gate_up_proj', 'down_proj')}
    del _L0_ffn_all

    def _L1_xattn_setup():
        import jax, jax.numpy as jnp
        import numpy as np
        B, S, H = (8, 256, 64)
        key = jax.random.key(seed)
        kq, kk, kqc, kwq, kwk = jax.random.split(key, 5)
        q = jax.random.normal(kq, (B, S, H), dtype=jnp.float32)
        k = jax.random.normal(kk, (B, S, H), dtype=jnp.float32)
        qc_score = jax.random.uniform(kqc, (B, S, S), dtype=jnp.float32)
        attn_mask = jnp.triu(jnp.ones((S, S), dtype=bool), k=1)
        key_padding_mask = jnp.zeros((B, S), dtype=bool)
        scale = 1.0 / np.sqrt(H)
        Wq = jax.random.normal(kwq, (H, H), dtype=jnp.float32) * scale
        Wk = jax.random.normal(kwk, (H, H), dtype=jnp.float32) * scale
        bq = jnp.zeros((H,), dtype=jnp.float32)
        bk = jnp.zeros((H,), dtype=jnp.float32)
        return {'q': q, 'k': k, 'attn_mask': attn_mask, 'key_padding_mask': key_padding_mask, 'qc_score': qc_score, 'Wq': Wq, 'bq': bq, 'Wk': Wk, 'bk': bk}
    _L1_xattn_all = _L1_xattn_setup()
    _L1_xattn_in = {k: v for k, v in _L1_xattn_all.items() if k in ('Wq', 'bq', 'Wk', 'bk')}
    del _L1_xattn_all

    def _L1_ffn_setup():
        import jax, jax.numpy as jnp
        import numpy as np
        NUM_EXPERTS = 64
        TOP_K = 8
        HIDDEN = 256
        INTER = 96
        key = jax.random.key(seed)
        k1, k2, k3, k4, k5 = jax.random.split(key, 5)
        hidden_states = jax.random.normal(k1, (4, 32, HIDDEN), dtype=jnp.float32)
        gate_w = jax.random.normal(k2, (HIDDEN, NUM_EXPERTS), dtype=jnp.float32) * 0.02
        w_gate = jax.random.normal(k3, (NUM_EXPERTS, HIDDEN, INTER), dtype=jnp.float32) * 0.02
        w_up = jax.random.normal(k4, (NUM_EXPERTS, HIDDEN, INTER), dtype=jnp.float32) * 0.02
        w_down = jax.random.normal(k5, (NUM_EXPERTS, INTER, HIDDEN), dtype=jnp.float32) * 0.02
        return {'hidden_states': hidden_states, 'gate_w': gate_w, 'w_gate': w_gate, 'w_up': w_up, 'w_down': w_down}
    _L1_ffn_all = _L1_ffn_setup()
    _L1_ffn_in = {k: v for k, v in _L1_ffn_all.items() if k in ('gate_w', 'w_gate', 'w_up', 'w_down')}
    del _L1_ffn_all
    return {'x': x, 'ctx_512': ctx_512, 'mask_SxS2_bk1': mask_SxS2_bk1, 'mask_BxS2_bf0': mask_BxS2_bf0, 'g_xattn': g_xattn, 'g_ffn': g_ffn, 'L0_xattn_Wq': _L0_xattn_in['Wq'], 'L0_xattn_Wk': _L0_xattn_in['Wk'], 'L0_xattn_gamma_raw': _L0_xattn_in['gamma_raw'], 'L0_ffn_gate_up_proj': _L0_ffn_in['gate_up_proj'], 'L0_ffn_down_proj': _L0_ffn_in['down_proj'], 'L1_xattn_Wq': _L1_xattn_in['Wq'], 'L1_xattn_bq': _L1_xattn_in['bq'], 'L1_xattn_Wk': _L1_xattn_in['Wk'], 'L1_xattn_bk': _L1_xattn_in['bk'], 'L1_ffn_gate_w': _L1_ffn_in['gate_w'], 'L1_ffn_w_gate': _L1_ffn_in['w_gate'], 'L1_ffn_w_up': _L1_ffn_in['w_up'], 'L1_ffn_w_down': _L1_ffn_in['w_down']}

def reference(x, ctx_512, mask_SxS2_bk1, mask_BxS2_bf0, g_xattn, g_ffn, L0_xattn_Wq, L0_xattn_Wk, L0_xattn_gamma_raw, L0_ffn_gate_up_proj, L0_ffn_down_proj, L1_xattn_Wq, L1_xattn_bq, L1_xattn_Wk, L1_xattn_bk, L1_ffn_gate_w, L1_ffn_w_gate, L1_ffn_w_up, L1_ffn_w_down):
    import jax
    import jax.numpy as jnp

    def _L0_xattn_ref(h, adj_raw, Wq, Wk, gamma_raw):
        import jax, jax.numpy as jnp
        import numpy as np
        B, N, D = (16, 256, 64)
        H = 4
        TOP_K_RATIO = 0.3
        b, n, dm = h.shape
        d = dm // H
        Q = (h @ Wq.T).reshape(b, n, H, d).transpose(0, 2, 1, 3)
        K = (h @ Wk.T).reshape(b, n, H, d).transpose(0, 2, 1, 3)
        sim = jnp.einsum('bhnd,bhmd->bnm', Q, K) / (jnp.sqrt(jnp.float32(d)) * H)
        k = max(1, int(n * TOP_K_RATIO))
        topk_vals = jax.lax.top_k(sim, k)[0]
        threshold = topk_vals[:, :, -1:]
        sparse_mask = (sim >= threshold).astype(sim.dtype)
        A_learned = jax.nn.sigmoid(sim) * sparse_mask
        A_learned = (A_learned + jnp.swapaxes(A_learned, -1, -2)) * 0.5
        gamma = jax.nn.sigmoid(gamma_raw)
        return (1.0 - gamma) * adj_raw + gamma * A_learned

    def _L0_ffn_ref(x, gate_up_proj, down_proj):
        import jax, jax.numpy as jnp
        import numpy as np
        NUM_EXPERTS = 4
        B, N, H = x.shape
        E, _, two_I = gate_up_proj.shape
        I = two_I // 2
        G = N // E
        x4 = x.reshape(B, G, E, H)
        gu = jnp.einsum('bgeh,ehd->bged', x4, gate_up_proj)
        gate, up = (gu[..., :I], gu[..., I:])
        inter = jax.nn.silu(gate) * up
        out = jnp.einsum('bgei,eih->bgeh', inter, down_proj)
        return out.reshape(B, N, H)

    def _L1_xattn_ref(q, k, attn_mask, key_padding_mask, qc_score, Wq, bq, Wk, bk):
        import jax, jax.numpy as jnp
        import numpy as np
        B, S, H = (8, 256, 64)
        qp = jnp.einsum('bsh,oh->bso', q, Wq) + bq
        kp = jnp.einsum('bth,oh->bto', k, Wk) + bk
        scaling = jnp.asarray(float(H) ** (-0.5), dtype=qp.dtype)
        scores = jnp.einsum('bsh,bth->bst', qp, kp) * scaling
        scores = scores * qc_score
        mask = attn_mask[None, :, :] | key_padding_mask[:, None, :]
        scores = jnp.where(mask, -jnp.inf, scores)
        return jax.nn.softmax(scores, axis=-1)

    def _L1_ffn_ref(hidden_states, gate_w, w_gate, w_up, w_down):
        import jax, jax.numpy as jnp
        import numpy as np
        NUM_EXPERTS = 64
        TOP_K = 8
        HIDDEN = 256
        INTER = 96
        orig_shape = hidden_states.shape
        x = hidden_states.reshape(-1, orig_shape[-1])
        T = x.shape[0]
        router_logits = x @ gate_w
        probs = jax.nn.softmax(router_logits.astype(jnp.float32), axis=-1)
        top_vals, top_idx = jax.lax.top_k(probs, TOP_K)
        top_vals = top_vals / jnp.sum(top_vals, axis=-1, keepdims=True)
        rw = jnp.zeros((T, NUM_EXPERTS), dtype=x.dtype)
        rw = rw.at[jnp.arange(T)[:, None], top_idx].set(top_vals)
        g = jnp.einsum('th,ehi->tei', x, w_gate)
        u = jnp.einsum('th,ehi->tei', x, w_up)
        h = jax.nn.silu(g) * u
        h = h * rw[:, :, None]
        out = jnp.einsum('tei,eih->th', h, w_down)
        return out.reshape(orig_shape)
    x = x + jnp.tanh(g_xattn[0]) * _L0_xattn_ref(ctx_512, _layernorm(x, axis=-1), L0_xattn_Wq, L0_xattn_Wk, L0_xattn_gamma_raw)
    x = x + jnp.tanh(g_ffn[0]) * _L0_ffn_ref(_layernorm(x, axis=-1), L0_ffn_gate_up_proj, L0_ffn_down_proj)
    x = x + jnp.tanh(g_xattn[1]) * _L1_xattn_ref(ctx_512, ctx_512, mask_SxS2_bk1, mask_BxS2_bf0, _layernorm(x, axis=-1), L1_xattn_Wq, L1_xattn_bq, L1_xattn_Wk, L1_xattn_bk)
    x = x + jnp.tanh(g_ffn[1]) * _L1_ffn_ref(_layernorm(x, axis=-1), L1_ffn_gate_w, L1_ffn_w_gate, L1_ffn_w_up, L1_ffn_w_down)
    return x

_drawn_inputs = setup_inputs


def setup_inputs(seed=0):
    import zlib

    import numpy as np

    out = dict(_drawn_inputs(seed))
    spreads = {'g_ffn': (-1.0, 0.6), 'L1_xattn_bq': (0.0, 0.8), 'L1_xattn_bk': (0.0, 0.8)}
    factors = {'L0_ffn_gate_up_proj': 4.312,
     'L0_ffn_down_proj': 4.308,
     'L1_xattn_Wq': 3.083,
     'L1_xattn_Wk': 3.114,
     'L1_ffn_gate_w': 8.0,
     'L1_ffn_w_gate': 8.0,
     'L1_ffn_w_up': 8.0,
     'L1_ffn_w_down': 8.0}
    for name, (base, spread) in spreads.items():
        noise = np.random.default_rng([zlib.crc32(name.encode()), seed]).standard_normal(out[name].shape)
        drawn = base * np.exp(spread * noise) if base else spread * noise
        out[name] = jnp.asarray(drawn.astype(out[name].dtype))
    for name, factor in factors.items():
        out[name] = (out[name] * factor).astype(out[name].dtype)
    return out
```

```python
from contextlib import ExitStack

import concourse.bass as bass
from concourse import mybir

F32 = mybir.dt.float32
U8 = mybir.dt.uint8
ALU = mybir.AluOpType
ACT = mybir.ActivationFunctionType

P = 128
EPS = 1e-5
TOP_K_RATIO = 0.3
HEADS0 = 4
TOP_K_EXPERTS = 8
MASKED = -1e35
REMOVED = -3e38
N_BANKS = 8
BANK = 512


def gated_layers_kernel(nc, x, ctx_in, mask_ss, mask_bs, g_xattn, g_ffn, wq0, wk0, gamma_raw, gate_up, down,
                        wq1, bq1, wk1, bk1, router_w, w_gate, w_up, w_down, out):
    B, S, D = x.shape
    C = ctx_in.shape[2]
    NT = B * S // P
    HB = S // P
    NE0, _, GU = gate_up.shape
    I0 = GU // 2
    KC = D // P
    IC = I0 // P
    T = B * S
    NE, _, I1 = w_gate.shape
    HALF = T // 2
    TOPK = max(1, int(S * TOP_K_RATIO))
    ROUNDS = -(-TOPK // 8)
    SIM_SCALE = 1.0 / (float(C // HEADS0) ** 0.5 * HEADS0)
    SCORE_SCALE = float(C) ** -0.5

    x_f = x.rearrange("b s d -> (b s) d").rearrange("(t p) d -> p t d", p=P)
    out_f = out.rearrange("b s d -> (b s) d").rearrange("(t p) d -> p t d", p=P)
    ctx_f = ctx_in.rearrange("b s d -> (b s) d").rearrange("(t p) d -> p t d", p=P)
    rw_dram = nc.dram_tensor("routing_weights_t", [NE, T], F32, kind="Internal").ap()

    with ExitStack() as stack:
        def sb(name, shape, dt=F32):
            return stack.enter_context(nc.sbuf_tensor(name, shape, dt))

        def sem(name):
            return stack.enter_context(nc.semaphore(name))

        ident = sb("ident", [P, P])
        xs = sb("xs", [P, NT, D])
        ctx_rows = sb("ctx_rows", [P, NT, C])
        ctx_t = sb("ctx_t", [C, T])
        w_rows = sb("w_rows", [C, 4, C])
        w_t = sb("w_t", [C, 4, C])
        bias1 = sb("bias1", [C, 2])
        proj_t = sb("proj_t", [C, 4, T])
        sim = sb("sim", [P, NT, S])
        work = sb("work", [P, NT, S])
        top8 = sb("top8", [P, NT, ROUNDS, 8])
        adj = sb("adj", [P, NT, S])
        scores = sb("scores", [P, NT, S])
        mask_s8 = sb("mask_s8", [P, HB, S], U8)
        mask_b8 = sb("mask_b8", [P, B, S], U8)
        pen_s = sb("pen_s", [P, HB, S])
        pen_b = sb("pen_b", [P, B, S])
        pen = sb("pen", [P, NT, S])
        gates = sb("gates", [P, 5])
        tg = sb("tg", [P, 4])
        gam = sb("gam", [P, 1])
        coef = sb("coef", [P, 4])
        stats = sb("stats", [P, NT, 6])
        mv = sb("mv", [P, 4, NT, 2])
        var_eps = sb("var_eps", [P, 4, NT])
        rstd = sb("rstd", [P, 4, NT])
        minus_half = sb("minus_half", [P, NT])
        a_scale = sb("a_scale", [P, NT])
        a_shift = sb("a_shift", [P, NT])
        base = sb("base", [P, NT, D])
        xn = sb("xn", [P, NT, D])
        xn_t = sb("xn_t", [P, KC, T])
        gu_w = sb("gu_w", [P, NE0, KC, GU])
        down_w = sb("down_w", [P, NE0, IC, D])
        silu0 = sb("silu0", [P, 2, BANK])
        h0_t = sb("h0_t", [P, 2, IC, T // NE0])
        y0_t = sb("y0_t", [P, KC, T])
        row_max = sb("row_max", [P, NT])
        exp_bias = sb("exp_bias", [P, NT])
        row_sum = sb("row_sum", [P, NT])
        inv_sum = sb("inv_sum", [P, NT])
        live = sb("live", [P, NT])
        router = sb("router", [P, KC, NE])
        l_max = sb("l_max", [P, NT, 8])
        l_neg = sb("l_neg", [P, NT])
        e_top = sb("e_top", [P, NT, 8])
        e_val = sb("e_val", [P, NT, NE])
        e_rest = sb("e_rest", [P, NT, NE])
        rw = sb("rw", [P, NT, NE])
        rw_t = sb("rw_t", [NE, T])
        wg = sb("wg", [P, 2, KC, I1])
        wu = sb("wu", [P, 2, KC, I1])
        wd = sb("wd", [I1, 2, D])
        rwb = sb("rwb", [I1, 2, T])
        zeros = sb("zeros", [P, BANK])
        silu1 = sb("silu1", [I1, 2, HALF])
        h1_t = sb("h1_t", [I1, 2, T])
        psum = stack.enter_context(nc.psum_tensor("psum", [P, N_BANKS, BANK], F32))

        ld = {n: sem("ld_" + n) for n in ("x", "ctx", "w", "bias", "gates", "ms", "mb", "gu", "down", "router")}
        ident_zero, ident_ready = sem("ident_zero"), sem("ident_ready")
        bank_filled = sem("bank_filled")
        act_evac, dve_evac = sem("act_evac"), sem("dve_evac")
        tanh_ready = sem("tanh_ready")
        coef_ready = sem("coef_ready")
        dve_step = sem("dve_step")
        pen_step, pen_ready = sem("pen_step"), sem("pen_ready")
        topk_ready, sig_ready, adj_ready = sem("topk_ready"), sem("sig_ready"), sem("adj_ready")
        base_ready = sem("base_ready")
        var_ready, eps_added, rstd_ready = sem("var_ready"), sem("eps_added"), sem("rstd_ready")
        ab_ready = sem("ab_ready")
        xn_ready = sem("xn_ready")
        silu0_ready, h0_ready = sem("silu0_ready"), sem("h0_ready")
        ebias_ready, exp_ready = sem("ebias_ready"), sem("exp_ready")
        l_neg_ready, e_ready, rw_ready = sem("l_neg_ready"), sem("e_ready"), sem("rw_ready")
        rw_stored, x3_ready = sem("rw_stored"), sem("x3_ready")
        w_landed = [sem("w_landed0"), sem("w_landed1")]
        w_used, gu_filled, up_used = sem("w_used"), sem("gu_filled"), sem("up_used")
        zeros_ready = sem("zeros_ready")
        silu1_ready, h_ready = sem("silu1_ready"), sem("h_ready")
        acc_done, out_ready, stored = sem("acc_done"), sem("out_ready"), sem("stored")

        fills = []

        def add_fill(name, engine):
            fills.append((name, engine))
            return len(fills) - 1

        F_CTX = [add_fill("ctx", "act"), add_fill("ctx", "dve")]
        F_W = add_fill("w", "dve")
        F_PROJ = [add_fill("proj", "act" if i % 2 else "dve") for i in range(4 * 2)]
        F_SIM = [add_fill("sim", "act" if i % 2 else "dve") for i in range(B)]
        F_SCORE = [add_fill("score", "act") for i in range(B)]
        F_ADJT = [add_fill("adjt", "dve") for i in range(B)]
        F_XNT = [add_fill("xnt", "act" if i % 2 else "dve") for i in range(B)]
        F_GU = []
        F_DOWN = []
        for e in range(NE0):
            F_GU.append((add_fill("gate", "act"), add_fill("up", "dve")))
            if e:
                F_DOWN.append(add_fill("down", "act"))
        F_DOWN.append(add_fill("down", "act"))
        F_YT = [add_fill("yt", "dve") for i in range(B)]
        F_XNT2 = [add_fill("xnt2", "act" if i % 2 else "dve") for i in range(B)]
        F_LOGIT = [add_fill("logit", "act") for i in range(B)]
        F_RWT = [add_fill("rwt", "act" if i % 2 else "dve") for i in range(2)]

        def emptied(eng, i):
            who = fills[i][1]
            n = sum(1 for f in fills[:i + 1] if f[1] == who)
            eng.wait_ge(act_evac if who == "act" else dve_evac, n)

        def bank(i):
            return psum[:, i % N_BANKS, :]

        def xn_t_view(k, b, permuted):
            if permuted:
                return xn_t[:, k].rearrange("p (e b g) -> p e b g", e=NE0, b=B)[:, :, b, :]
            return xn_t[:, k, b * S:(b + 1) * S]

        def xn_bank_view(i, k, permuted):
            src = bank(i)[:, k * S:(k + 1) * S]
            return src.rearrange("p (g e) -> p e g", e=NE0) if permuted else src

        block = stack.enter_context(nc.Block())

        @block.sync
        def _(sp):
            sp.dma_start(ctx_rows[:], ctx_f).then_inc(ld["ctx"], 16)
            for i, w in enumerate((wq0, wk0, wq1, wk1)):
                sp.dma_start(w_rows[:, i, :], w).then_inc(ld["w"], 16)
            sp.dma_start(bias1[:, 0:1], bq1.rearrange("(c a) -> c a", a=1)).then_inc(ld["bias"], 16)
            sp.dma_start(bias1[:, 1:2], bk1.rearrange("(c a) -> c a", a=1)).then_inc(ld["bias"], 16)
            sp.dma_start(xs[:], x_f).then_inc(ld["x"], 16)
            sp.dma_start(gates[:, 0:2], g_xattn.rearrange("(a n) -> a n", a=1).to_broadcast([P, 2])).then_inc(ld["gates"], 16)
            sp.dma_start(gates[:, 2:4], g_ffn.rearrange("(a n) -> a n", a=1).to_broadcast([P, 2])).then_inc(ld["gates"], 16)
            sp.dma_start(gates[:, 4:5], gamma_raw.to_broadcast([P, 1])).then_inc(ld["gates"], 16)
            sp.dma_start(mask_s8[:], mask_ss.rearrange("(h p) m -> p h m", p=P)).then_inc(ld["ms"], 16)
            sp.dma_start(mask_b8[:].rearrange("p b s -> p (b s)"), mask_bs.rearrange("(a b) s -> a (b s)", a=1).to_broadcast([P, B * S])).then_inc(ld["mb"], 16)
            for e in range(NE0):
                sp.dma_start(gu_w[:, e], gate_up[e].rearrange("(k p) n -> p k n", p=P)).then_inc(ld["gu"], 16)
            for e in range(NE0):
                sp.dma_start(down_w[:, e], down[e].rearrange("(k p) n -> p k n", p=P)).then_inc(ld["down"], 16)
            sp.dma_start(router[:], router_w.rearrange("(k p) n -> p k n", p=P)).then_inc(ld["router"], 16)
            emptied(sp, F_RWT[0])
            emptied(sp, F_RWT[1])
            sp.dma_start(rw_dram, rw_t[:]).then_inc(rw_stored, 16)
            sp.wait_ge(rw_stored, 16)

            def load(e, k, used):
                if used is not None:
                    sp.wait_ge(w_used, used)
                sp.dma_start(wg[:, k], w_gate[bass.ds(e, 1)].rearrange("a (k p) n -> p (a k) n", p=P)).then_inc(w_landed[k], 16)
                sp.dma_start(wu[:, k], w_up[bass.ds(e, 1)].rearrange("a (k p) n -> p (a k) n", p=P)).then_inc(w_landed[k], 16)
                sp.dma_start(wd[:, k], w_down[bass.ds(e, 1)].rearrange("a p n -> p (a n)")).then_inc(w_landed[k], 16)
                sp.dma_start(rwb[:, k], rw_dram[bass.ds(e, 1), :].to_broadcast([I1, T])).then_inc(w_landed[k], 16)

            load(0, 0, None)
            load(1, 1, None)
            with sp.Fori(1, NE // 2) as i:
                load(2 * i, 0, 2 * i - 1)
                load(2 * i + 1, 1, 2 * i)
            sp.wait_ge(out_ready, NT // 2)
            sp.dma_start(out_f, xs[:]).then_inc(stored, 16)
            sp.wait_ge(stored, 16)

        @block.gpsimd
        def _(pool):
            pool.memset(ident[:], 0.0).then_inc(ident_zero, 1)
            pool.wait_ge(ident_zero, 1)
            pool.affine_select(out=ident[:], in_=ident[:], compare_op=ALU.not_equal, fill=1.0, base=0,
                               pattern=[[-1, P]], channel_multiplier=1).then_inc(ident_ready, 1)
            pool.memset(zeros[:], 0.0).then_inc(zeros_ready, 1)
            pool.memset(minus_half[:], -0.5).then_inc(pen_step, 1)
            pool.wait_ge(ld["ms"], 16)
            pool.tensor_scalar(pen_s[:], mask_s8[:], MASKED, None, ALU.mult).then_inc(pen_step, 1)
            pool.wait_ge(ld["mb"], 16)
            pool.tensor_scalar(pen_b[:], mask_b8[:], MASKED, None, ALU.mult).then_inc(pen_step, 1)
            pool.wait_ge(pen_step, 3)

            def inverse_deviation(n):
                pool.wait_ge(var_ready, NT * (n + 1))
                pool.tensor_scalar(var_eps[:, n], mv[:, n, :, 1], EPS, None, ALU.add).then_inc(eps_added, 1)
                pool.wait_ge(eps_added, n + 1)
                pool.tensor_tensor(rstd[:, n], var_eps[:, n], minus_half[:], ALU.pow).then_inc(rstd_ready, 1)

            inverse_deviation(0)
            for b in range(B):
                for h in range(HB):
                    pool.tensor_tensor(pen[:, b * HB + h], pen_s[:, h], pen_b[:, b], ALU.add).then_inc(pen_ready, 1)
            for n in range(1, 4):
                inverse_deviation(n)

        @block.tensor
        def _(pe):
            def begin(i):
                if i >= N_BANKS:
                    emptied(pe, i - N_BANKS)

            pe.wait_ge(ident_ready, 1)
            pe.wait_ge(ld["ctx"], 16)
            for half in range(2):
                i = F_CTX[half]
                begin(i)
                for t in range(NT // 2):
                    last = pe.transpose(bank(i)[0:C, t * P:(t + 1) * P], ctx_rows[:, half * (NT // 2) + t, :], ident[:])
                last.then_inc(bank_filled, 1)
            pe.wait_ge(ld["w"], 64)
            for i in range(4):
                last = pe.transpose(bank(F_W)[0:C, i * C:(i + 1) * C], w_rows[:, i, :], ident[0:C, 0:C])
            last.then_inc(bank_filled, 1)
            emptied(pe, F_CTX[0])
            emptied(pe, F_CTX[1])
            emptied(pe, F_W)
            for w in range(4):
                for half in range(2):
                    i = F_PROJ[w * 2 + half]
                    begin(i)
                    pe.matmul(bank(i)[0:C, :], w_t[:, w, :], ctx_t[:, half * HALF:(half + 1) * HALF],
                              start=True, stop=True).then_inc(bank_filled, 1)
            for layer, fill in ((0, F_SIM), (1, F_SCORE)):
                for n in range(4):
                    emptied(pe, F_PROJ[layer * 4 + n])
                for b in range(B):
                    i = fill[b]
                    begin(i)
                    for h in range(HB):
                        t = b * HB + h
                        last = pe.matmul(bank(i)[:, h * S:(h + 1) * S], proj_t[:, 2 * layer, t * P:(t + 1) * P],
                                         proj_t[:, 2 * layer + 1, b * S:(b + 1) * S], start=True, stop=True)
                    last.then_inc(bank_filled, 1)
            for b in range(B):
                i = F_ADJT[b]
                begin(i)
                pe.wait_ge(adj_ready, HB * (b + 1))
                for h in range(HB):
                    for m in range(HB):
                        last = pe.transpose(bank(i)[:, h * S + m * P:h * S + (m + 1) * P],
                                            adj[:, b * HB + m, h * P:(h + 1) * P], ident[:])
                last.then_inc(bank_filled, 1)

            def transpose_normed(fill, ready):
                for b in range(B):
                    i = fill[b]
                    begin(i)
                    pe.wait_ge(xn_ready, ready + HB * (b + 1))
                    for k in range(KC):
                        for h in range(HB):
                            last = pe.transpose(bank(i)[:, k * S + h * P:k * S + (h + 1) * P],
                                                xn[:, b * HB + h, k * P:(k + 1) * P], ident[:])
                    last.then_inc(bank_filled, 1)
                for b in range(B):
                    emptied(pe, fill[b])

            transpose_normed(F_XNT, 0)
            pe.wait_ge(ld["gu"], 16 * NE0)
            pe.wait_ge(ld["down"], 16 * NE0)
            TE = T // NE0

            def expert_down0(e):
                i = F_DOWN[e]
                begin(i)
                pe.wait_ge(h0_ready, e + 1)
                for hc in range(KC):
                    for ic in range(IC):
                        last = pe.matmul(bank(i)[:, hc * TE:(hc + 1) * TE], down_w[:, e, ic, hc * P:(hc + 1) * P],
                                         h0_t[:, e % 2, ic, :], start=ic == 0, stop=ic == IC - 1)
                last.then_inc(bank_filled, 1)

            for e in range(NE0):
                for part in range(2):
                    i = F_GU[e][part]
                    begin(i)
                    for ic in range(IC):
                        for k in range(KC):
                            c = part * I0 + ic * P
                            last = pe.matmul(bank(i)[:, ic * TE:(ic + 1) * TE], gu_w[:, e, k, c:c + P],
                                             xn_t[:, k, e * TE:(e + 1) * TE], start=k == 0, stop=k == KC - 1)
                    last.then_inc(bank_filled, 1)
                if e:
                    expert_down0(e - 1)
            expert_down0(NE0 - 1)
            for e in range(NE0):
                emptied(pe, F_DOWN[e])
            for b in range(B):
                i = F_YT[b]
                begin(i)
                for h in range(HB):
                    for k in range(KC):
                        t = b * HB + h
                        last = pe.transpose(bank(i)[:, h * D + k * P:h * D + (k + 1) * P],
                                            y0_t[:, k, t * P:(t + 1) * P], ident[:])
                last.then_inc(bank_filled, 1)
            transpose_normed(F_XNT2, NT)
            pe.wait_ge(ld["router"], 16)
            for b in range(B):
                i = F_LOGIT[b]
                begin(i)
                for h in range(HB):
                    t = b * HB + h
                    for k in range(KC):
                        last = pe.matmul(bank(i)[:, h * NE:(h + 1) * NE], xn_t[:, k, t * P:(t + 1) * P], router[:, k, :],
                                         start=k == 0, stop=k == KC - 1)
                last.then_inc(bank_filled, 1)
            for half in range(2):
                i = F_RWT[half]
                begin(i)
                pe.wait_ge(rw_ready, (half + 1) * NT // 2)
                for t in range(NT // 2):
                    last = pe.transpose(bank(i)[0:NE, t * P:(t + 1) * P], rw[:, half * NT // 2 + t, :], ident[:])
                last.then_inc(bank_filled, 1)
            emptied(pe, F_RWT[0])
            emptied(pe, F_RWT[1])
            emptied(pe, F_LOGIT[B - 1])

            pe.wait_ge(zeros_ready, 1)
            for n in range(4):
                pe.matmul(psum[:, 4 + n, :], zeros[:, 0:P], zeros[:], start=True, stop=False, skip_group_check=True)

            def gate_up1(e, k, pair, first=False):
                pe.wait_ge(w_landed[k], 64 * pair + 64)
                for half in range(2):
                    if not first:
                        pe.wait_ge(up_used, 2 * e + half - 1)
                    for part, w in enumerate((wg, wu)):
                        for c in range(KC):
                            last = pe.matmul(psum[0:I1, 2 * half + part, :], w[:, k, c, :],
                                             xn_t[:, c, half * HALF:(half + 1) * HALF],
                                             start=c == 0, stop=c == KC - 1)
                    last.then_inc(gu_filled, 1)

            def down1(e, k, signal=None):
                pe.wait_ge(h_ready, 2 * e + 2)
                for t in range(NT):
                    last = pe.matmul(psum[:, 4 + t // 2, (t % 2) * D:(t % 2 + 1) * D], h1_t[:, k, t * P:(t + 1) * P],
                                     wd[:, k, :], start=False, stop=signal is not None, skip_group_check=True)
                last.then_inc(signal or w_used, 1)

            gate_up1(0, 0, 0, first=True)
            gate_up1(1, 1, 0)
            down1(0, 0)
            with pe.Fori(1, NE // 2) as i:
                gate_up1(2 * i, 0, i)
                down1(2 * i - 1, 1)
                gate_up1(2 * i + 1, 1, i)
                down1(2 * i, 0)
            down1(NE - 1, 1, acc_done)

        @block.scalar
        def _(act):
            act.wait_ge(ld["gates"], 48)
            act.activation(tg[:], gates[:, 0:4], ACT.Tanh).then_inc(tanh_ready, 1)
            act.activation(gam[:], gates[:, 4:5], ACT.Sigmoid).then_inc(tanh_ready, 1)

            def filled(i):
                act.wait_ge(bank_filled, i + 1)

            filled(F_CTX[0])
            act.copy(ctx_t[:, 0:HALF], bank(F_CTX[0])[0:C, :]).then_inc(act_evac, 1)
            for n in (1, 3, 5, 7):
                w, half = n // 2, n % 2
                i = F_PROJ[n]
                filled(i)
                dst = proj_t[:, w, half * HALF:(half + 1) * HALF]
                if w < 2:
                    act.copy(dst, bank(i)[0:C, :]).then_inc(act_evac, 1)
                else:
                    act.wait_ge(ld["bias"], 32)
                    act.activation(dst, bank(i)[0:C, :], ACT.Identity, bias=bias1[:, w - 2:w - 1]).then_inc(act_evac, 1)
            for b in (1, 3):
                filled(F_SIM[b])
                act.mul(sim[:, b * HB:(b + 1) * HB, :].rearrange("p h s -> p (h s)"), bank(F_SIM[b]), SIM_SCALE).then_inc(act_evac, 1)
            for b in range(B):
                filled(F_SCORE[b])
                act.mul(scores[:, b * HB:(b + 1) * HB, :].rearrange("p h s -> p (h s)"), bank(F_SCORE[b]), SCORE_SCALE).then_inc(act_evac, 1)
            for b in range(B):
                emptied(act, F_SIM[b])
                act.activation(adj[:, b * HB:(b + 1) * HB, :], sim[:, b * HB:(b + 1) * HB, :], ACT.Sigmoid).then_inc(sig_ready, 1)
            act.wait_ge(ab_ready, 1)
            for t in range(NT):
                act.activation(base[:, t], xs[:, t], ACT.Identity, bias=a_shift[:, t:t + 1], scale=a_scale[:, t:t + 1]).then_inc(base_ready, 1)

            def evacuate_xnt(fill, permuted):
                for b in (1, 3):
                    filled(fill[b])
                    for k in range(KC):
                        last = act.copy(xn_t_view(k, b, permuted), xn_bank_view(fill[b], k, permuted))
                    last.then_inc(act_evac, 1)

            evacuate_xnt(F_XNT, True)

            def evacuate_down(e):
                filled(F_DOWN[e])
                for k in range(KC):
                    last = act.copy(y0_t[:, k].rearrange("p (n e) -> p e n", e=NE0)[:, e],
                                    bank(F_DOWN[e])[:, k * (T // NE0):(k + 1) * (T // NE0)])
                last.then_inc(act_evac, 1)

            for e in range(NE0):
                filled(F_GU[e][0])
                if e >= 2:
                    act.wait_ge(h0_ready, e - 1)
                act.activation(silu0[:, e % 2], bank(F_GU[e][0]), ACT.Silu).then_inc(act_evac, 1)
                if e:
                    evacuate_down(e - 1)
            evacuate_down(NE0 - 1)
            for t in range(NT):
                act.wait_ge(ebias_ready, t + 1)
                act.activation(work[:, t], work[:, t], ACT.Exp, bias=exp_bias[:, t:t + 1], scale=rstd[:, 2, t:t + 1],
                               accum_out=row_sum[:, t:t + 1]).then_inc(exp_ready, 1)
            evacuate_xnt(F_XNT2, False)
            for b in range(B):
                filled(F_LOGIT[b])
                act.copy(e_rest[:, b * HB:(b + 1) * HB].rearrange("p h n -> p (h n)"), bank(F_LOGIT[b])[:, 0:HB * NE]).then_inc(act_evac, 1)
            for t in range(NT):
                act.wait_ge(l_neg_ready, 1)
                act.activation(e_val[:, t], e_rest[:, t], ACT.Exp, bias=l_neg[:, t:t + 1]).then_inc(e_ready, 1)
            filled(F_RWT[1])
            act.copy(rw_t[:, HALF:T], bank(F_RWT[1])[0:NE, :]).then_inc(act_evac, 1)

            def silu_halves(e):
                for half in range(2):
                    act.wait_ge(gu_filled, 2 * e + half + 1)
                    act.activation(silu1[:, half], psum[0:I1, 2 * half, :], ACT.Silu).then_inc(silu1_ready, 1)

            with act.Fori(0, NE) as e:
                silu_halves(e)

        @block.vector
        def _(dve):
            steps = [0]

            def link(ins):
                steps[0] += 1
                ins.then_inc(dve_step, 1)
                dve.wait_ge(dve_step, steps[0])

            def filled(i):
                dve.wait_ge(bank_filled, i + 1)

            def statistics(n):
                for t in range(NT):
                    last = dve.bn_stats(stats[:, t], xs[:, t])
                link(last)
                for t in range(NT):
                    dve.bn_aggr(mv[:, n, t], stats[:, t]).then_inc(var_ready, 1)

            filled(F_CTX[1])
            dve.tensor_copy(ctx_t[:, HALF:T], bank(F_CTX[1])[0:C, :]).then_inc(dve_evac, 1)
            filled(F_W)
            dve.tensor_copy(w_t[:].rearrange("p w c -> p (w c)"), bank(F_W)[0:C, 0:4 * C]).then_inc(dve_evac, 1)
            for n in (0, 2, 4, 6):
                w, half = n // 2, n % 2
                i = F_PROJ[n]
                filled(i)
                dst = proj_t[:, w, half * HALF:(half + 1) * HALF]
                if w < 2:
                    dve.tensor_copy(dst, bank(i)[0:C, :]).then_inc(dve_evac, 1)
                else:
                    dve.wait_ge(ld["bias"], 32)
                    dve.tensor_scalar(dst, bank(i)[0:C, :], bias1[:, w - 2:w - 1], None, ALU.add).then_inc(dve_evac, 1)
            for b in (0, 2):
                filled(F_SIM[b])
                dve.tensor_scalar(sim[:, b * HB:(b + 1) * HB, :].rearrange("p h s -> p (h s)"), bank(F_SIM[b]), SIM_SCALE, None,
                                  ALU.mult).then_inc(dve_evac, 1)
            dve.wait_ge(ld["x"], 16)
            statistics(0)
            dve.wait_ge(tanh_ready, 2)
            link(dve.tensor_tensor(coef[:, 0:1], tg[:, 0:1], gam[:], ALU.mult))
            link(dve.tensor_scalar(coef[:, 1:2], coef[:, 0:1], 0.5, None, ALU.mult))
            link(dve.tensor_tensor(coef[:, 2:3], tg[:, 0:1], coef[:, 0:1], ALU.subtract))
            dve.wait_ge(rstd_ready, 1)
            dve.wait_ge(var_ready, NT)
            link(dve.tensor_scalar(a_shift[:], rstd[:, 0], coef[:, 2:3], -1.0, ALU.mult, ALU.mult))
            link(dve.tensor_scalar(a_scale[:], a_shift[:], -1.0, 1.0, ALU.mult, ALU.add))
            dve.tensor_tensor(a_shift[:], a_shift[:], mv[:, 0, :, 0], ALU.mult).then_inc(ab_ready, 1)
            for t in range(NT):
                emptied(dve, F_SIM[t // HB])
                for r in range(ROUNDS):
                    src = sim if r == 0 else work
                    link(dve.max(top8[:, t, r], src[:, t]))
                    if r < ROUNDS - 1:
                        link(dve.match_replace(work[:, t], top8[:, t, r], src[:, t], REMOVED))
                dve.wait_ge(sig_ready, t // HB + 1)
                kth = top8[:, t, (TOPK - 1) // 8, (TOPK - 1) % 8:(TOPK - 1) % 8 + 1]
                dve.scalar_tensor_tensor(out=adj[:, t], in0=sim[:, t], scalar=kth, in1=adj[:, t], op0=ALU.is_ge,
                                         op1=ALU.mult).then_inc(adj_ready, 1)
            for b in range(B):
                two = slice(b * HB, (b + 1) * HB)
                filled(F_ADJT[b])
                dve.tensor_tensor(adj[:, two].rearrange("p h s -> p (h s)"), adj[:, two].rearrange("p h s -> p (h s)"),
                                  bank(F_ADJT[b]), ALU.add).then_inc(dve_evac, 1)
                emptied(dve, F_ADJT[b])
                dve.wait_ge(base_ready, HB * (b + 1))
                last = dve.scalar_tensor_tensor(out=xs[:, two], in0=adj[:, two], scalar=coef[:, 1:2], in1=base[:, two],
                                                op0=ALU.mult, op1=ALU.add)
            link(last)

            def normalise(n):
                dve.wait_ge(rstd_ready, n + 1)
                for t in range(NT):
                    dve.tensor_scalar(xn[:, t], xs[:, t], mv[:, n, t, 0:1], rstd[:, n, t:t + 1], ALU.subtract,
                                      ALU.mult).then_inc(xn_ready, 1)

            def evacuate_xnt(fill, permuted):
                for b in (0, 2):
                    filled(fill[b])
                    for k in range(KC):
                        last = dve.tensor_copy(xn_t_view(k, b, permuted), xn_bank_view(fill[b], k, permuted))
                    last.then_inc(dve_evac, 1)

            statistics(1)
            dve.wait_ge(var_ready, 2 * NT)
            normalise(1)
            evacuate_xnt(F_XNT, True)
            for e in range(NE0):
                emptied(dve, F_GU[e][0])
                filled(F_GU[e][1])
                if e >= 2:
                    dve.wait_ge(bank_filled, F_DOWN[e - 2] + 1)
                dve.tensor_tensor(h0_t[:, e % 2].rearrange("p i t -> p (i t)"), silu0[:, e % 2], bank(F_GU[e][1]),
                                  ALU.mult).then_inc(dve_evac, 1)
                emptied(dve, F_GU[e][1])
                dve.sem_inc(h0_ready, 1)
            for b in range(B):
                two = slice(b * HB, (b + 1) * HB)
                filled(F_YT[b])
                last = dve.scalar_tensor_tensor(out=xs[:, two].rearrange("p h s -> p (h s)"), in0=bank(F_YT[b]),
                                                scalar=tg[:, 2:3], in1=xs[:, two].rearrange("p h s -> p (h s)"),
                                                op0=ALU.mult, op1=ALU.add).then_inc(dve_evac, 1)
            emptied(dve, F_YT[B - 1])
            statistics(2)
            dve.wait_ge(rstd_ready, 3)
            dve.wait_ge(var_ready, 3 * NT)
            emptied(dve, F_SCORE[B - 1])
            dve.wait_ge(pen_ready, NT)
            for t in range(NT):
                link(dve.scalar_tensor_tensor(out=work[:, t], in0=xs[:, t], scalar=mv[:, 2, t, 0:1], in1=scores[:, t],
                                              op0=ALU.subtract, op1=ALU.mult))
                link(dve.tensor_tensor_reduce(out=work[:, t], in0=work[:, t], in1=pen[:, t], scale=1.0, scalar=2 * MASKED,
                                              op0=ALU.add, op1=ALU.max, accum_out=row_max[:, t:t + 1]))
                dve.scalar_tensor_tensor(out=exp_bias[:, t:t + 1], in0=row_max[:, t:t + 1], scalar=-1.0,
                                         in1=rstd[:, 2, t:t + 1], op0=ALU.mult, op1=ALU.mult).then_inc(ebias_ready, 1)
            link(dve.tensor_scalar(live[:], row_max[:], MASKED / 2, None, ALU.is_gt))
            dve.wait_ge(exp_ready, NT)
            link(dve.tensor_tensor(row_sum[:], row_sum[:], live[:], ALU.mult))
            link(dve.reciprocal(inv_sum[:], row_sum[:]))
            link(dve.scalar_tensor_tensor(out=inv_sum[:], in0=inv_sum[:], scalar=tg[:, 1:2], in1=live[:], op0=ALU.mult, op1=ALU.mult))
            for t in range(NT):
                last = dve.scalar_tensor_tensor(out=xs[:, t], in0=work[:, t], scalar=inv_sum[:, t:t + 1], in1=xs[:, t],
                                                op0=ALU.mult, op1=ALU.add)
            link(last)
            statistics(3)
            dve.wait_ge(var_ready, 4 * NT)
            normalise(3)
            evacuate_xnt(F_XNT2, False)
            emptied(dve, F_LOGIT[B - 1])
            for t in range(NT):
                last = dve.max(l_max[:, t], e_rest[:, t])
            link(last)
            dve.tensor_scalar(l_neg[:], l_max[:, :, 0], -1.0, None, ALU.mult).then_inc(l_neg_ready, 1)
            for t in range(NT):
                dve.wait_ge(e_ready, t + 1)
                link(dve.max(e_top[:, t], e_val[:, t]))
                link(dve.match_replace(e_rest[:, t], e_top[:, t], e_val[:, t], -1.0))
                link(dve.scalar_tensor_tensor(out=e_rest[:, t], in0=e_rest[:, t], scalar=0.0, in1=e_val[:, t], op0=ALU.is_lt,
                                              op1=ALU.mult, accum_out=l_neg[:, t:t + 1]))
                link(dve.reciprocal(l_max[:, t, 0:1], l_neg[:, t:t + 1]))
                dve.tensor_scalar(rw[:, t], e_rest[:, t], l_max[:, t, 0:1], None, ALU.mult).then_inc(rw_ready, 1)
            filled(F_RWT[0])
            dve.tensor_copy(rw_t[:, 0:HALF], bank(F_RWT[0])[0:NE, :]).then_inc(dve_evac, 1)

            def weigh(e, k, pair, first):
                dve.wait_ge(w_landed[k], 64 * pair + 64)
                if not first:
                    dve.wait_ge(w_used, e - 1)
                for half in range(2):
                    dve.wait_ge(silu1_ready, 2 * e + half + 1)
                    cols = slice(half * HALF, (half + 1) * HALF)
                    dve.tensor_tensor(h1_t[:, k, cols], silu1[:, half], psum[0:I1, 2 * half + 1, :], ALU.mult).then_inc(up_used, 1)
                    dve.wait_ge(up_used, 2 * e + half + 1)
                    dve.tensor_tensor(h1_t[:, k, cols], h1_t[:, k, cols], rwb[:, k, cols], ALU.mult).then_inc(h_ready, 1)

            weigh(0, 0, 0, True)
            weigh(1, 1, 0, True)
            with dve.Fori(1, NE // 2) as i:
                weigh(2 * i, 0, i, False)
                weigh(2 * i + 1, 1, i, False)
            dve.wait_ge(acc_done, 1)
            for n in range(NT // 2):
                two = xs[:, 2 * n:2 * n + 2].rearrange("p h s -> p (h s)")
                dve.scalar_tensor_tensor(out=two, in0=psum[:, 4 + n, :], scalar=tg[:, 3:4], in1=two, op0=ALU.mult,
                                         op1=ALU.add).then_inc(out_ready, 1)


_INS = ["x", "ctx_512", "mask_SxS2_bk1", "mask_BxS2_bf0", "g_xattn", "g_ffn", "L0_xattn_Wq", "L0_xattn_Wk",
        "L0_xattn_gamma_raw", "L0_ffn_gate_up_proj", "L0_ffn_down_proj", "L1_xattn_Wq", "L1_xattn_bq", "L1_xattn_Wk",
        "L1_xattn_bk", "L1_ffn_gate_w", "L1_ffn_w_gate", "L1_ffn_w_up", "L1_ffn_w_down"]


def kernel(**inputs):
    import numpy as _np
    import concourse.bacc as _bacc
    from concourse import mybir as _mybir
    from concourse.bass_utils import run_bass_kernel_spmd as _run

    nc = _bacc.Bacc("TRN2", target_bir_lowering=False, num_devices=1)
    arrays, args = {}, []
    for name in _INS:
        a = _np.ascontiguousarray(inputs[name])
        if a.ndim == 0:
            a = a.reshape(1, 1)
        arrays[f"in_{name}"] = a
        args.append(nc.dram_tensor(f"in_{name}", a.shape, _mybir.dt.from_np(a.dtype), kind="ExternalInput").ap())
    x = arrays["in_x"]
    out = nc.dram_tensor("out_0", x.shape, _mybir.dt.from_np(x.dtype), kind="ExternalOutput").ap()
    gated_layers_kernel(nc, *args, out)
    r = _run(nc, [arrays], core_ids=[0])
    return r.results[0]["out_0"]
```

```python
from contextlib import ExitStack

import concourse.bass as bass
from concourse import mybir

F32 = mybir.dt.float32
U8 = mybir.dt.uint8
BF16 = mybir.dt.bfloat16
F16 = mybir.dt.float16
I32 = mybir.dt.int32
U32 = mybir.dt.uint32
ALU = mybir.AluOpType
ACT = mybir.ActivationFunctionType

P = 128
EPS = 1e-5
TOP_K_RATIO = 0.3
HEADS0 = 4
TOP_K_EXPERTS = 8
MASKED = -1e35
REMOVED = -3e38
N_BANKS = 8
BANK = 512
LANES = 4
PARTS = 3
W_SCALE = 4096.0
N_COLS = 1 + PARTS
N_SUMS = 4


def gated_layers_kernel(nc, x, ctx_in, mask_ss, mask_bs, g_xattn, g_ffn, wq0, wk0, gamma_raw, gate_up, down,
                        wq1, bq1, wk1, bk1, router_w, w_gate, w_up, w_down, out):
    B, S, D = x.shape
    C = ctx_in.shape[2]
    NT = B * S // P
    HB = S // P
    NE0, _, GU = gate_up.shape
    I0 = GU // 2
    KC = D // P
    IC = I0 // P
    T = B * S
    NE, _, I1 = w_gate.shape
    HALF = T // 2
    TOPK = max(1, int(S * TOP_K_RATIO))
    ROUNDS = -(-TOPK // 8)
    SIM_SCALE = 1.0 / (float(C // HEADS0) ** 0.5 * HEADS0)
    SCORE_SCALE = float(C) ** -0.5

    x_f = x.rearrange("b s d -> (b s) d").rearrange("(t p) d -> p t d", p=P)
    out_f = out.rearrange("b s d -> (b s) d").rearrange("(t p) d -> p t d", p=P)
    ctx_f = ctx_in.rearrange("b s d -> (b s) d").rearrange("(t p) d -> p t d", p=P)
    MIN_QUADS = T * TOP_K_EXPERTS // P // LANES
    MAX_QUADS = P // LANES
    MAX_COUNT_TILES = T // P
    xn_dram = nc.dram_tensor("normed_rows", [T + P, D], F32, kind="Internal").ap()
    sums_dram = [nc.dram_tensor(f"expert_sums{n}", [T + P, D], F32, kind="Internal").ap() for n in range(N_SUMS)]

    with ExitStack() as stack:
        def sb(name, shape, dt=F32):
            return stack.enter_context(nc.sbuf_tensor(name, shape, dt))

        def sem(name):
            return stack.enter_context(nc.semaphore(name))

        ident = sb("ident", [P, P])
        xs = sb("xs", [P, NT, D])
        ctx_rows = sb("ctx_rows", [P, NT, C])
        ctx_t = sb("ctx_t", [C, T])
        w_rows = sb("w_rows", [C, 4, C])
        w_t = sb("w_t", [C, 4, C])
        bias1 = sb("bias1", [C, 2])
        proj_t = sb("proj_t", [C, 4, T])
        sim = sb("sim", [P, NT, S])
        work = sb("work", [P, NT, S])
        top8 = sb("top8", [P, NT, ROUNDS, 8])
        adj = sb("adj", [P, NT, S])
        scores = sb("scores", [P, NT, S])
        mask_s8 = sb("mask_s8", [P, HB, S], U8)
        mask_b8 = sb("mask_b8", [P, B, S], U8)
        pen_s = sb("pen_s", [P, HB, S])
        pen_b = sb("pen_b", [P, B, S])
        pen = sb("pen", [P, NT, S])
        gates = sb("gates", [P, 5])
        tg = sb("tg", [P, 4])
        gam = sb("gam", [P, 1])
        coef = sb("coef", [P, 4])
        stats = sb("stats", [P, NT, 6])
        mv = sb("mv", [P, 4, NT, 2])
        var_eps = sb("var_eps", [P, 4, NT])
        rstd = sb("rstd", [P, 4, NT])
        minus_half = sb("minus_half", [P, NT])
        a_scale = sb("a_scale", [P, NT])
        a_shift = sb("a_shift", [P, NT])
        base = sb("base", [P, NT, D])
        xn = sb("xn", [P, NT, D])
        xn_t = sb("xn_t", [P, KC, T])
        gu_w = sb("gu_w", [P, NE0, KC, GU])
        down_w = sb("down_w", [P, NE0, IC, D])
        silu0 = sb("silu0", [P, 2, BANK])
        h0_t = sb("h0_t", [P, 2, IC, T // NE0])
        y0_t = sb("y0_t", [P, KC, T])
        row_max = sb("row_max", [P, NT])
        exp_bias = sb("exp_bias", [P, NT])
        row_sum = sb("row_sum", [P, NT])
        inv_sum = sb("inv_sum", [P, NT])
        live = sb("live", [P, NT])
        router = sb("router", [P, KC, NE])
        l_max = sb("l_max", [P, NT, 8])
        l_neg = sb("l_neg", [P, NT])
        e_top = sb("e_top", [P, NT, 8])
        e_val = sb("e_val", [P, NT, NE])
        e_rest = sb("e_rest", [P, NT, NE])
        rw = sb("rw", [P, NT, NE])
        zeros = sb("zeros", [P, 2 * BANK])
        chosen = sb("chosen", [P, NT, NE], BF16)
        before = sb("before", [P, P], BF16)
        ones_b = sb("ones_b", [P, P], BF16)
        ones_f = sb("ones_f", [P, P])
        rank = sb("rank", [P, NT, NE])
        w_rest = sb("w_rest", [P, NT, NE])
        w_parts = sb("w_parts", [P, NT, NE, PARTS], F16)
        n_tiles = sb("n_tiles", [P, NE])
        n_tiles_i = sb("n_tiles_i", [P, 2, NE], I32)
        tiles_end = sb("tiles_end", [P, NE])
        list_scratch = sb("list_scratch", [P, 2, NE])
        row_id = sb("row_id", [P, 1])
        empty_row = sb("empty_row", [P, 1])
        token_id = sb("token_id", [P, NT])
        slot_id = sb("slot_id", [P, NT, P], F16)
        tile_of = sb("tile_of", [P, 4])
        tile_diag = sb("tile_diag", [P, 2, P])
        first_rank = sb("first_rank", [P, P])
        expert_of = sb("expert_of", [1, P], I32)
        n_quads = sb("n_quads", [1, 4], I32)
        local = sb("local", [P, 2, NT], F16)
        one_hot = sb("one_hot", [P, 2, NT, P], F16)
        cols = sb("cols", [P, 2, NT, N_COLS], F16)
        w_seen = sb("w_seen", [P, 2, PARTS])
        slot_w = sb("slot_w", [P, LANES])
        gather_at = sb("gather_at", [P, LANES], U32)
        scatter_at = sb("scatter_at", [P, LANES], U32)
        x_slots = sb("x_slots", [P, LANES, D])
        x_slots_t = sb("x_slots_t", [P, 2, KC, P])
        wg = sb("wg", [P, LANES, KC, I1])
        wu = sb("wu", [P, LANES, KC, I1])
        wd = sb("wd", [I1, LANES, D])
        silu1 = sb("silu1", [I1, 2, P])
        h1_t = sb("h1_t", [I1, 2, P])
        y_slots = sb("y_slots", [P, LANES, D])
        psum = stack.enter_context(nc.psum_tensor("psum", [P, N_BANKS, BANK], F32))

        ld = {n: sem("ld_" + n) for n in ("x", "ctx", "w", "bias", "gates", "ms", "mb", "gu", "down", "router")}
        ident_zero, ident_ready = sem("ident_zero"), sem("ident_ready")
        bank_filled = sem("bank_filled")
        act_evac, dve_evac = sem("act_evac"), sem("dve_evac")
        tanh_ready = sem("tanh_ready")
        coef_ready = sem("coef_ready")
        dve_step = sem("dve_step")
        pen_step, pen_ready = sem("pen_step"), sem("pen_ready")
        topk_ready, sig_ready, adj_ready = sem("topk_ready"), sem("sig_ready"), sem("adj_ready")
        base_ready = sem("base_ready")
        var_ready, eps_added, rstd_ready = sem("var_ready"), sem("eps_added"), sem("rstd_ready")
        ab_ready = sem("ab_ready")
        xn_ready = sem("xn_ready")
        silu0_ready, h0_ready = sem("silu0_ready"), sem("h0_ready")
        ebias_ready, exp_ready = sem("ebias_ready"), sem("exp_ready")
        l_neg_ready, e_ready, rw_ready = sem("l_neg_ready"), sem("e_ready"), sem("rw_ready")
        zeros_ready, consts_ready = sem("zeros_ready"), sem("consts_ready")
        scratch_zeroed, x3_ready, x3_stored, xn_stored = sem("scratch_zeroed"), sem("x3_ready"), sem("x3_stored"), sem("xn_stored")
        chosen_ready, diag_ready, lists_ready = sem("chosen_ready"), sem("diag_ready"), sem("lists_ready")
        cols_ready, list_filled, list_copied = sem("cols_ready"), sem("list_filled"), sem("list_copied")
        gathered = [sem(f"gathered{n}") for n in range(LANES)]
        w_landed = [sem(f"w_landed{n}") for n in range(LANES)]
        scattered = [sem(f"scattered{n}") for n in range(N_SUMS)]
        xt_filled, xt_copied, gu_filled = sem("xt_filled"), sem("xt_copied"), sem("gu_filled")
        silu1_ready, h_ready, y_filled, y_ready = sem("silu1_ready"), sem("h_ready"), sem("y_filled"), sem("y_ready")
        local_ready = sem("local_ready")
        gathers_begun, scatters_begun = sem("gathers_begun"), sem("scatters_begun")
        sums_loaded, out_ready, stored = sem("sums_loaded"), sem("out_ready"), sem("stored")

        fills = []

        def add_fill(name, engine):
            fills.append((name, engine))
            return len(fills) - 1

        F_CTX = [add_fill("ctx", "act"), add_fill("ctx", "dve")]
        F_W = add_fill("w", "dve")
        F_PROJ = [add_fill("proj", "act" if i % 2 else "dve") for i in range(4 * 2)]
        F_SIM = [add_fill("sim", "act" if i % 2 else "dve") for i in range(B)]
        F_SCORE = [add_fill("score", "act") for i in range(B)]
        F_ADJT = [add_fill("adjt", "dve") for i in range(B)]
        F_XNT = [add_fill("xnt", "act" if i % 2 else "dve") for i in range(B)]
        F_GU = []
        F_DOWN = []
        for e in range(NE0):
            F_GU.append((add_fill("gate", "act"), add_fill("up", "dve")))
            if e:
                F_DOWN.append(add_fill("down", "act"))
        F_DOWN.append(add_fill("down", "act"))
        F_YT = [add_fill("yt", "dve") for i in range(B)]
        F_XNT2 = [add_fill("xnt2", "act" if i % 2 else "dve") for i in range(B)]
        F_LOGIT = [add_fill("logit", "act") for i in range(B)]
        F_RANK = add_fill("rank", "dve")
        F_COUNT = add_fill("count", "dve")
        F_TILES = add_fill("tiles", "dve")

        def emptied(eng, i):
            who = fills[i][1]
            n = sum(1 for f in fills[:i + 1] if f[1] == who)
            eng.wait_ge(act_evac if who == "act" else dve_evac, n)

        def bank(i):
            return psum[:, i % N_BANKS, :]

        def xn_t_view(k, b, permuted):
            if permuted:
                return xn_t[:, k].rearrange("p (e b g) -> p e b g", e=NE0, b=B)[:, :, b, :]
            return xn_t[:, k, b * S:(b + 1) * S]

        def xn_bank_view(i, k, permuted):
            src = bank(i)[:, k * S:(k + 1) * S]
            return src.rearrange("p (g e) -> p e g", e=NE0) if permuted else src

        def need(eng, semaphore, n):
            if not (isinstance(n, int) and n <= 0):
                eng.wait_ge(semaphore, n)

        class Tile:

            def __init__(self, quad, lane):
                self.quad, self.lane = quad, lane
                self.j = quad * LANES + lane
                self.two = lane % 2

            def later(self, n):
                return Tile(self.quad + (self.lane + n) // LANES, (self.lane + n) % LANES)

        def over_tiles(eng, slot):
            eng.wait_ge(lists_ready, 1)
            inner_quads = eng.value_load(n_quads[0:1, 0:1], min_val=MIN_QUADS - 2, max_val=MAX_QUADS - 2)
            for lane in range(LANES):
                slot(Tile(0, lane), None)
            with eng.Fori(1, inner_quads + 1) as quad:
                for lane in range(LANES):
                    slot(Tile(quad, lane), None)
            for lane in range(LANES):
                slot(Tile(inner_quads + 1, lane), LANES - 1 - lane)
            return inner_quads + 1

        block = stack.enter_context(nc.Block())

        @block.sync
        def _(sp):
            sp.dma_start(ctx_rows[:], ctx_f).then_inc(ld["ctx"], 16)
            for i, w in enumerate((wq0, wk0, wq1, wk1)):
                sp.dma_start(w_rows[:, i, :], w).then_inc(ld["w"], 16)
            sp.dma_start(bias1[:, 0:1], bq1.rearrange("(c a) -> c a", a=1)).then_inc(ld["bias"], 16)
            sp.dma_start(bias1[:, 1:2], bk1.rearrange("(c a) -> c a", a=1)).then_inc(ld["bias"], 16)
            sp.dma_start(xs[:], x_f).then_inc(ld["x"], 16)
            sp.dma_start(gates[:, 0:2], g_xattn.rearrange("(a n) -> a n", a=1).to_broadcast([P, 2])).then_inc(ld["gates"], 16)
            sp.dma_start(gates[:, 2:4], g_ffn.rearrange("(a n) -> a n", a=1).to_broadcast([P, 2])).then_inc(ld["gates"], 16)
            sp.dma_start(gates[:, 4:5], gamma_raw.to_broadcast([P, 1])).then_inc(ld["gates"], 16)
            sp.dma_start(mask_s8[:], mask_ss.rearrange("(h p) m -> p h m", p=P)).then_inc(ld["ms"], 16)
            sp.dma_start(mask_b8[:].rearrange("p b s -> p (b s)"), mask_bs.rearrange("(a b) s -> a (b s)", a=1).to_broadcast([P, B * S])).then_inc(ld["mb"], 16)
            for e in range(NE0):
                sp.dma_start(gu_w[:, e], gate_up[e].rearrange("(k p) n -> p k n", p=P)).then_inc(ld["gu"], 16)
            for e in range(NE0):
                sp.dma_start(down_w[:, e], down[e].rearrange("(k p) n -> p k n", p=P)).then_inc(ld["down"], 16)
            sp.dma_start(router[:], router_w.rearrange("(k p) n -> p k n", p=P)).then_inc(ld["router"], 16)
            sp.wait_ge(zeros_ready, 1)
            z_rows = zeros[:, 0:2 * BANK].rearrange("p (r d) -> p r d", d=D)
            for rows in sums_dram[1:]:
                for n in range(NT // 4):
                    sp.dma_start(rows[n * 4 * P:(n + 1) * 4 * P, :].rearrange("(p r) d -> p r d", p=P), z_rows).then_inc(scratch_zeroed, 16)
            for rows in (*sums_dram, xn_dram):
                sp.dma_start(rows[T:T + P, :], zeros[:, 0:D]).then_inc(scratch_zeroed, 16)
            sp.wait_ge(x3_ready, 1)
            sp.dma_start(sums_dram[0][0:T, :].rearrange("(t p) d -> p t d", p=P), xs[:]).then_inc(x3_stored, 16)
            sp.wait_ge(xn_ready, 2 * NT)
            sp.dma_start(xn_dram[0:T, :].rearrange("(t p) d -> p t d", p=P), xn[:]).then_inc(xn_stored, 16)

            def load_weights(tile, left):
                need(sp, y_filled, tile.j - LANES + 1)
                e = sp.value_load(expert_of[0:1, bass.ds(tile.j, 1)], min_val=0, max_val=NE - 1)
                n = tile.lane
                sp.dma_start(wg[:, n], w_gate[bass.ds(e, 1)].rearrange("a (p k) n -> p (a k) n", p=P)).then_inc(w_landed[n], 16)
                sp.dma_start(wu[:, n], w_up[bass.ds(e, 1)].rearrange("a (p k) n -> p (a k) n", p=P)).then_inc(w_landed[n], 16)
                sp.dma_start(wd[:, n], w_down[bass.ds(e, 1)].rearrange("a p n -> p (a n)")).then_inc(w_landed[n], 16)

            last_quad = over_tiles(sp, load_weights)
            for n in range(N_SUMS):
                sp.wait_ge(scattered[n], last_quad * 16 + 16)
                sp.dma_start((base, adj, sim, work)[n][:], sums_dram[n][0:T, :].rearrange("(t p) d -> p t d", p=P)).then_inc(sums_loaded, 16)
            sp.wait_ge(out_ready, 1)
            sp.dma_start(out_f, xs[:]).then_inc(stored, 16)
            sp.wait_ge(stored, 16)

        @block.gpsimd
        def _(pool):
            pool.memset(ident[:], 0.0).then_inc(ident_zero, 1)
            pool.wait_ge(ident_zero, 1)
            pool.affine_select(out=ident[:], in_=ident[:], compare_op=ALU.not_equal, fill=1.0, base=0,
                               pattern=[[-1, P]], channel_multiplier=1).then_inc(ident_ready, 1)
            pool.memset(zeros[:], 0.0).then_inc(zeros_ready, 1)
            pool.memset(minus_half[:], -0.5).then_inc(pen_step, 1)
            pool.memset(ones_b[:], 1.0).then_inc(consts_ready, 1)
            pool.memset(ones_f[:], 1.0).then_inc(consts_ready, 1)
            pool.iota(row_id[:], [[0, 1]], base=0, channel_multiplier=1, allow_small_or_imprecise_dtypes=True).then_inc(consts_ready, 1)
            pool.iota(empty_row[:], [[0, 1]], base=T, channel_multiplier=1, allow_small_or_imprecise_dtypes=True).then_inc(consts_ready, 1)
            pool.iota(slot_id[:], [[0, NT], [1, P]], base=0, channel_multiplier=0, allow_small_or_imprecise_dtypes=True).then_inc(consts_ready, 1)
            pool.iota(token_id[:], [[P, NT]], base=-T, channel_multiplier=1, allow_small_or_imprecise_dtypes=True).then_inc(consts_ready, 1)
            pool.wait_ge(consts_ready, 6)
            pool.affine_select(out=before[:], in_=ones_b[:], compare_op=ALU.is_gt, fill=0.0, base=0,
                               pattern=[[1, P]], channel_multiplier=-1).then_inc(consts_ready, 1)
            pool.wait_ge(ld["ms"], 16)
            pool.tensor_scalar(pen_s[:], mask_s8[:], MASKED, None, ALU.mult).then_inc(pen_step, 1)
            pool.wait_ge(ld["mb"], 16)
            pool.tensor_scalar(pen_b[:], mask_b8[:], MASKED, None, ALU.mult).then_inc(pen_step, 1)
            pool.wait_ge(pen_step, 3)

            def inverse_deviation(n):
                pool.wait_ge(var_ready, NT * (n + 1))
                pool.tensor_scalar(var_eps[:, n], mv[:, n, :, 1], EPS, None, ALU.add).then_inc(eps_added, 1)
                pool.wait_ge(eps_added, n + 1)
                pool.tensor_tensor(rstd[:, n], var_eps[:, n], minus_half[:], ALU.pow).then_inc(rstd_ready, 1)

            inverse_deviation(0)
            for b in range(B):
                for h in range(HB):
                    pool.tensor_tensor(pen[:, b * HB + h], pen_s[:, h], pen_b[:, b], ALU.add).then_inc(pen_ready, 1)
            for n in range(1, 4):
                inverse_deviation(n)

            pool.wait_ge(scratch_zeroed, 16 * ((N_SUMS - 1) * NT // 4 + N_SUMS + 1))
            pool.wait_ge(x3_stored, 16)
            pool.wait_ge(xn_stored, 16)

            def gather(tile):
                need(pool, xt_filled, tile.j - LANES + 1)
                pool.wait_ge(list_copied, tile.j + 1)
                pool.sem_inc(gathers_begun, 1)
                pool.indirect_dma_start(x_slots[:, tile.lane, :], None, xn_dram,
                                        bass.IndirectOffsetOnAxis(ap=gather_at[:, tile.lane:tile.lane + 1], axis=0)).then_inc(gathered[tile.lane], 16)

            def scatter(tile):
                pool.wait_ge(y_ready, tile.j + 1)
                need(pool, scattered[tile.lane], tile.quad * 16)
                pool.sem_inc(scatters_begun, 1)
                pool.indirect_dma_start(sums_dram[tile.lane], bass.IndirectOffsetOnAxis(ap=scatter_at[:, tile.lane:tile.lane + 1], axis=0),
                                        y_slots[:, tile.lane, :], None, compute_op=ALU.add).then_inc(scattered[tile.lane], 16)

            def slot(tile, left):
                if left is None or left >= 3:
                    gather(tile.later(3))
                scatter(tile)

            for n in range(3):
                gather(Tile(0, n))
            over_tiles(pool, slot)

        @block.tensor
        def _(pe):
            def begin(i):
                if i >= N_BANKS:
                    emptied(pe, i - N_BANKS)

            pe.wait_ge(ident_ready, 1)
            pe.wait_ge(ld["ctx"], 16)
            for half in range(2):
                i = F_CTX[half]
                begin(i)
                for t in range(NT // 2):
                    last = pe.transpose(bank(i)[0:C, t * P:(t + 1) * P], ctx_rows[:, half * (NT // 2) + t, :], ident[:])
                last.then_inc(bank_filled, 1)
            pe.wait_ge(ld["w"], 64)
            for i in range(4):
                last = pe.transpose(bank(F_W)[0:C, i * C:(i + 1) * C], w_rows[:, i, :], ident[0:C, 0:C])
            last.then_inc(bank_filled, 1)
            emptied(pe, F_CTX[0])
            emptied(pe, F_CTX[1])
            emptied(pe, F_W)
            for w in range(4):
                for half in range(2):
                    i = F_PROJ[w * 2 + half]
                    begin(i)
                    pe.matmul(bank(i)[0:C, :], w_t[:, w, :], ctx_t[:, half * HALF:(half + 1) * HALF],
                              start=True, stop=True).then_inc(bank_filled, 1)
            for layer, fill in ((0, F_SIM), (1, F_SCORE)):
                for n in range(4):
                    emptied(pe, F_PROJ[layer * 4 + n])
                for b in range(B):
                    i = fill[b]
                    begin(i)
                    for h in range(HB):
                        t = b * HB + h
                        last = pe.matmul(bank(i)[:, h * S:(h + 1) * S], proj_t[:, 2 * layer, t * P:(t + 1) * P],
                                         proj_t[:, 2 * layer + 1, b * S:(b + 1) * S], start=True, stop=True)
                    last.then_inc(bank_filled, 1)
            for b in range(B):
                i = F_ADJT[b]
                begin(i)
                pe.wait_ge(adj_ready, HB * (b + 1))
                for h in range(HB):
                    for m in range(HB):
                        last = pe.transpose(bank(i)[:, h * S + m * P:h * S + (m + 1) * P],
                                            adj[:, b * HB + m, h * P:(h + 1) * P], ident[:])
                last.then_inc(bank_filled, 1)

            def transpose_normed(fill, ready):
                for b in range(B):
                    i = fill[b]
                    begin(i)
                    pe.wait_ge(xn_ready, ready + HB * (b + 1))
                    for k in range(KC):
                        for h in range(HB):
                            last = pe.transpose(bank(i)[:, k * S + h * P:k * S + (h + 1) * P],
                                                xn[:, b * HB + h, k * P:(k + 1) * P], ident[:])
                    last.then_inc(bank_filled, 1)
                for b in range(B):
                    emptied(pe, fill[b])

            transpose_normed(F_XNT, 0)
            pe.wait_ge(ld["gu"], 16 * NE0)
            pe.wait_ge(ld["down"], 16 * NE0)
            TE = T // NE0

            def expert_down0(e):
                i = F_DOWN[e]
                begin(i)
                pe.wait_ge(h0_ready, e + 1)
                for hc in range(KC):
                    for ic in range(IC):
                        last = pe.matmul(bank(i)[:, hc * TE:(hc + 1) * TE], down_w[:, e, ic, hc * P:(hc + 1) * P],
                                         h0_t[:, e % 2, ic, :], start=ic == 0, stop=ic == IC - 1)
                last.then_inc(bank_filled, 1)

            for e in range(NE0):
                for part in range(2):
                    i = F_GU[e][part]
                    begin(i)
                    for ic in range(IC):
                        for k in range(KC):
                            c = part * I0 + ic * P
                            last = pe.matmul(bank(i)[:, ic * TE:(ic + 1) * TE], gu_w[:, e, k, c:c + P],
                                             xn_t[:, k, e * TE:(e + 1) * TE], start=k == 0, stop=k == KC - 1)
                    last.then_inc(bank_filled, 1)
                if e:
                    expert_down0(e - 1)
            expert_down0(NE0 - 1)
            for e in range(NE0):
                emptied(pe, F_DOWN[e])
            for b in range(B):
                i = F_YT[b]
                begin(i)
                for h in range(HB):
                    for k in range(KC):
                        t = b * HB + h
                        last = pe.transpose(bank(i)[:, h * D + k * P:h * D + (k + 1) * P],
                                            y0_t[:, k, t * P:(t + 1) * P], ident[:])
                last.then_inc(bank_filled, 1)
            transpose_normed(F_XNT2, NT)
            pe.wait_ge(ld["router"], 16)
            for b in range(B):
                i = F_LOGIT[b]
                begin(i)
                for h in range(HB):
                    t = b * HB + h
                    for k in range(KC):
                        last = pe.matmul(bank(i)[:, h * NE:(h + 1) * NE], xn_t[:, k, t * P:(t + 1) * P], router[:, k, :],
                                         start=k == 0, stop=k == KC - 1)
                last.then_inc(bank_filled, 1)
            pe.wait_ge(chosen_ready, 1)
            pe.wait_ge(consts_ready, 7)
            begin(F_RANK)
            rank_ps = bank(F_RANK).rearrange("p (t e) -> p t e", t=NT)
            pe.matmul(rank_ps, before[:], chosen[:], start=True, stop=False)
            for t in range(NT - 1):
                last = pe.matmul(rank_ps[:, t + 1:NT, :], ones_b[:], chosen[:, t:t + 1, :].to_broadcast([P, NT - 1 - t, NE]),
                                 start=False, stop=t == NT - 2)
            last.then_inc(bank_filled, 1)
            begin(F_COUNT)
            for t in range(NT):
                last = pe.matmul(bank(F_COUNT)[:, 0:NE], ones_b[:], chosen[:, t, :], start=t == 0, stop=t == NT - 1)
            last.then_inc(bank_filled, 1)
            begin(F_TILES)
            pe.wait_ge(diag_ready, 1)
            pe.matmul(bank(F_TILES)[:, 0:2 * P], ones_f[:], tile_diag[:].rearrange("p n j -> p (n j)"), start=True, stop=True).then_inc(bank_filled, 1)
            emptied(pe, F_TILES)
            emptied(pe, F_LOGIT[B - 1])

            def slot_lists(tile):
                pe.wait_ge(cols_ready, tile.j + 1)
                need(pe, list_copied, tile.j - 1)
                for t in range(NT):
                    last = pe.matmul(psum[:, tile.two, 0:N_COLS], one_hot[:, tile.two, t, :], cols[:, tile.two, t, :],
                                     start=t == 0, stop=t == NT - 1)
                last.then_inc(list_filled, 1)

            def transpose_slots(tile):
                pe.wait_ge(gathered[tile.lane], tile.quad * 16 + 16)
                need(pe, xt_copied, tile.j - 1)
                for k in range(KC):
                    last = pe.transpose(psum[:, 2 + tile.two, k * P:(k + 1) * P],
                                        x_slots[:, tile.lane, :].rearrange("p (n k) -> p k n", k=KC)[:, k, :], ident[:])
                last.then_inc(xt_filled, 1)

            def gate_up1(tile):
                pe.wait_ge(xt_copied, tile.j + 1)
                pe.wait_ge(w_landed[tile.lane], tile.quad * 48 + 48)
                need(pe, h_ready, tile.j - 1)
                for part, w in enumerate((wg, wu)):
                    for k in range(KC):
                        last = pe.matmul(psum[0:I1, 4 + tile.two, part * P:(part + 1) * P], w[:, tile.lane, k, :],
                                         x_slots_t[:, tile.two, k, :], start=k == 0, stop=k == KC - 1)
                last.then_inc(gu_filled, 1)

            def down1(tile):
                pe.wait_ge(h_ready, tile.j + 1)
                need(pe, y_ready, tile.j - 1)
                pe.matmul(psum[:, 6 + tile.two, 0:D], h1_t[:, tile.two, :], wd[:, tile.lane, :],
                          start=True, stop=True).then_inc(y_filled, 1)

            def slot(tile, left):
                gate_up1(tile)
                if left is None or left >= 3:
                    slot_lists(tile.later(3))
                if left is None or left >= 1:
                    transpose_slots(tile.later(1))
                down1(tile)

            for n in range(3):
                slot_lists(Tile(0, n))
            transpose_slots(Tile(0, 0))
            over_tiles(pe, slot)

        @block.scalar
        def _(act):
            act.wait_ge(ld["gates"], 48)
            act.activation(tg[:], gates[:, 0:4], ACT.Tanh).then_inc(tanh_ready, 1)
            act.activation(gam[:], gates[:, 4:5], ACT.Sigmoid).then_inc(tanh_ready, 1)

            def filled(i):
                act.wait_ge(bank_filled, i + 1)

            filled(F_CTX[0])
            act.copy(ctx_t[:, 0:HALF], bank(F_CTX[0])[0:C, :]).then_inc(act_evac, 1)
            for n in (1, 3, 5, 7):
                w, half = n // 2, n % 2
                i = F_PROJ[n]
                filled(i)
                dst = proj_t[:, w, half * HALF:(half + 1) * HALF]
                if w < 2:
                    act.copy(dst, bank(i)[0:C, :]).then_inc(act_evac, 1)
                else:
                    act.wait_ge(ld["bias"], 32)
                    act.activation(dst, bank(i)[0:C, :], ACT.Identity, bias=bias1[:, w - 2:w - 1]).then_inc(act_evac, 1)
            for b in (1, 3):
                filled(F_SIM[b])
                act.mul(sim[:, b * HB:(b + 1) * HB, :].rearrange("p h s -> p (h s)"), bank(F_SIM[b]), SIM_SCALE).then_inc(act_evac, 1)
            for b in range(B):
                filled(F_SCORE[b])
                act.mul(scores[:, b * HB:(b + 1) * HB, :].rearrange("p h s -> p (h s)"), bank(F_SCORE[b]), SCORE_SCALE).then_inc(act_evac, 1)
            for b in range(B):
                emptied(act, F_SIM[b])
                act.activation(adj[:, b * HB:(b + 1) * HB, :], sim[:, b * HB:(b + 1) * HB, :], ACT.Sigmoid).then_inc(sig_ready, 1)
            act.wait_ge(ab_ready, 1)
            for t in range(NT):
                act.activation(base[:, t], xs[:, t], ACT.Identity, bias=a_shift[:, t:t + 1], scale=a_scale[:, t:t + 1]).then_inc(base_ready, 1)

            def evacuate_xnt(fill, permuted):
                for b in (1, 3):
                    filled(fill[b])
                    for k in range(KC):
                        last = act.copy(xn_t_view(k, b, permuted), xn_bank_view(fill[b], k, permuted))
                    last.then_inc(act_evac, 1)

            evacuate_xnt(F_XNT, True)

            def evacuate_down(e):
                filled(F_DOWN[e])
                for k in range(KC):
                    last = act.copy(y0_t[:, k].rearrange("p (n e) -> p e n", e=NE0)[:, e],
                                    bank(F_DOWN[e])[:, k * (T // NE0):(k + 1) * (T // NE0)])
                last.then_inc(act_evac, 1)

            for e in range(NE0):
                filled(F_GU[e][0])
                if e >= 2:
                    act.wait_ge(h0_ready, e - 1)
                act.activation(silu0[:, e % 2], bank(F_GU[e][0]), ACT.Silu).then_inc(act_evac, 1)
                if e:
                    evacuate_down(e - 1)
            evacuate_down(NE0 - 1)
            for t in range(NT):
                act.wait_ge(ebias_ready, t + 1)
                act.activation(work[:, t], work[:, t], ACT.Exp, bias=exp_bias[:, t:t + 1], scale=rstd[:, 2, t:t + 1],
                               accum_out=row_sum[:, t:t + 1]).then_inc(exp_ready, 1)
            evacuate_xnt(F_XNT2, False)
            for b in range(B):
                filled(F_LOGIT[b])
                act.copy(e_rest[:, b * HB:(b + 1) * HB].rearrange("p h n -> p (h n)"), bank(F_LOGIT[b])[:, 0:HB * NE]).then_inc(act_evac, 1)
            for t in range(NT):
                act.wait_ge(l_neg_ready, 1)
                act.activation(e_val[:, t], e_rest[:, t], ACT.Exp, bias=l_neg[:, t:t + 1]).then_inc(e_ready, 1)

            def copy_lists(tile):
                n = tile.lane
                act.wait_ge(list_filled, tile.j + 1)
                need(act, gathered[n], tile.quad * 16)
                need(act, y_ready, tile.j - LANES + 1)
                act.activation(w_seen[:, tile.two], psum[:, tile.two, 1:N_COLS], ACT.Copy, scale=1.0 / W_SCALE,
                               accum_out=slot_w[:, n:n + 1])
                act.activation(gather_at[:, n:n + 1], psum[:, tile.two, 0:1], ACT.Identity, bias=empty_row[:]).then_inc(list_copied, 1)

            def copy_slots_t(tile):
                need(act, gu_filled, tile.j - 1)
                act.wait_ge(xt_filled, tile.j + 1)
                act.copy(x_slots_t[:, tile.two].rearrange("p k n -> p (k n)"), psum[:, 2 + tile.two, 0:D]).then_inc(xt_copied, 1)

            def slot(tile, left):
                act.wait_ge(gu_filled, tile.j + 1)
                need(act, h_ready, tile.j - 1)
                act.activation(silu1[:, tile.two], psum[0:I1, 4 + tile.two, 0:P], ACT.Silu).then_inc(silu1_ready, 1)
                if left is None or left >= 3:
                    copy_lists(tile.later(3))
                if left is None or left >= 1:
                    copy_slots_t(tile.later(1))
                act.wait_ge(y_filled, tile.j + 1)
                need(act, scattered[tile.lane], tile.quad * 16)
                act.copy(scatter_at[:, tile.lane:tile.lane + 1], gather_at[:, tile.lane:tile.lane + 1])
                act.activation(y_slots[:, tile.lane, :], psum[:, 6 + tile.two, 0:D], ACT.Copy,
                               scale=slot_w[:, tile.lane:tile.lane + 1]).then_inc(y_ready, 1)

            for n in range(3):
                copy_lists(Tile(0, n))
            copy_slots_t(Tile(0, 0))
            over_tiles(act, slot)

        @block.vector
        def _(dve):
            steps = [0]

            def link(ins):
                steps[0] += 1
                ins.then_inc(dve_step, 1)
                dve.wait_ge(dve_step, steps[0])

            def filled(i):
                dve.wait_ge(bank_filled, i + 1)

            def statistics(n):
                for t in range(NT):
                    last = dve.bn_stats(stats[:, t], xs[:, t])
                link(last)
                for t in range(NT):
                    dve.bn_aggr(mv[:, n, t], stats[:, t]).then_inc(var_ready, 1)

            filled(F_CTX[1])
            dve.tensor_copy(ctx_t[:, HALF:T], bank(F_CTX[1])[0:C, :]).then_inc(dve_evac, 1)
            filled(F_W)
            dve.tensor_copy(w_t[:].rearrange("p w c -> p (w c)"), bank(F_W)[0:C, 0:4 * C]).then_inc(dve_evac, 1)
            for n in (0, 2, 4, 6):
                w, half = n // 2, n % 2
                i = F_PROJ[n]
                filled(i)
                dst = proj_t[:, w, half * HALF:(half + 1) * HALF]
                if w < 2:
                    dve.tensor_copy(dst, bank(i)[0:C, :]).then_inc(dve_evac, 1)
                else:
                    dve.wait_ge(ld["bias"], 32)
                    dve.tensor_scalar(dst, bank(i)[0:C, :], bias1[:, w - 2:w - 1], None, ALU.add).then_inc(dve_evac, 1)
            for b in (0, 2):
                filled(F_SIM[b])
                dve.tensor_scalar(sim[:, b * HB:(b + 1) * HB, :].rearrange("p h s -> p (h s)"), bank(F_SIM[b]), SIM_SCALE, None,
                                  ALU.mult).then_inc(dve_evac, 1)
            dve.wait_ge(ld["x"], 16)
            statistics(0)
            dve.wait_ge(tanh_ready, 2)
            link(dve.tensor_tensor(coef[:, 0:1], tg[:, 0:1], gam[:], ALU.mult))
            link(dve.tensor_scalar(coef[:, 1:2], coef[:, 0:1], 0.5, None, ALU.mult))
            link(dve.tensor_tensor(coef[:, 2:3], tg[:, 0:1], coef[:, 0:1], ALU.subtract))
            dve.wait_ge(rstd_ready, 1)
            dve.wait_ge(var_ready, NT)
            link(dve.tensor_scalar(a_shift[:], rstd[:, 0], coef[:, 2:3], -1.0, ALU.mult, ALU.mult))
            link(dve.tensor_scalar(a_scale[:], a_shift[:], -1.0, 1.0, ALU.mult, ALU.add))
            dve.tensor_tensor(a_shift[:], a_shift[:], mv[:, 0, :, 0], ALU.mult).then_inc(ab_ready, 1)
            for t in range(NT):
                emptied(dve, F_SIM[t // HB])
                for r in range(ROUNDS):
                    src = sim if r == 0 else work
                    link(dve.max(top8[:, t, r], src[:, t]))
                    if r < ROUNDS - 1:
                        link(dve.match_replace(work[:, t], top8[:, t, r], src[:, t], REMOVED))
                dve.wait_ge(sig_ready, t // HB + 1)
                kth = top8[:, t, (TOPK - 1) // 8, (TOPK - 1) % 8:(TOPK - 1) % 8 + 1]
                dve.scalar_tensor_tensor(out=adj[:, t], in0=sim[:, t], scalar=kth, in1=adj[:, t], op0=ALU.is_ge,
                                         op1=ALU.mult).then_inc(adj_ready, 1)
            for b in range(B):
                two = slice(b * HB, (b + 1) * HB)
                filled(F_ADJT[b])
                dve.tensor_tensor(adj[:, two].rearrange("p h s -> p (h s)"), adj[:, two].rearrange("p h s -> p (h s)"),
                                  bank(F_ADJT[b]), ALU.add).then_inc(dve_evac, 1)
                emptied(dve, F_ADJT[b])
                dve.wait_ge(base_ready, HB * (b + 1))
                last = dve.scalar_tensor_tensor(out=xs[:, two], in0=adj[:, two], scalar=coef[:, 1:2], in1=base[:, two],
                                                op0=ALU.mult, op1=ALU.add)
            link(last)

            def normalise(n):
                dve.wait_ge(rstd_ready, n + 1)
                for t in range(NT):
                    dve.tensor_scalar(xn[:, t], xs[:, t], mv[:, n, t, 0:1], rstd[:, n, t:t + 1], ALU.subtract,
                                      ALU.mult).then_inc(xn_ready, 1)

            def evacuate_xnt(fill, permuted):
                for b in (0, 2):
                    filled(fill[b])
                    for k in range(KC):
                        last = dve.tensor_copy(xn_t_view(k, b, permuted), xn_bank_view(fill[b], k, permuted))
                    last.then_inc(dve_evac, 1)

            statistics(1)
            dve.wait_ge(var_ready, 2 * NT)
            normalise(1)
            evacuate_xnt(F_XNT, True)
            for e in range(NE0):
                emptied(dve, F_GU[e][0])
                filled(F_GU[e][1])
                if e >= 2:
                    dve.wait_ge(bank_filled, F_DOWN[e - 2] + 1)
                dve.tensor_tensor(h0_t[:, e % 2].rearrange("p i t -> p (i t)"), silu0[:, e % 2], bank(F_GU[e][1]),
                                  ALU.mult).then_inc(dve_evac, 1)
                emptied(dve, F_GU[e][1])
                dve.sem_inc(h0_ready, 1)
            for b in range(B):
                two = slice(b * HB, (b + 1) * HB)
                filled(F_YT[b])
                last = dve.scalar_tensor_tensor(out=xs[:, two].rearrange("p h s -> p (h s)"), in0=bank(F_YT[b]),
                                                scalar=tg[:, 2:3], in1=xs[:, two].rearrange("p h s -> p (h s)"),
                                                op0=ALU.mult, op1=ALU.add).then_inc(dve_evac, 1)
            emptied(dve, F_YT[B - 1])
            statistics(2)
            dve.wait_ge(rstd_ready, 3)
            dve.wait_ge(var_ready, 3 * NT)
            emptied(dve, F_SCORE[B - 1])
            dve.wait_ge(pen_ready, NT)
            for t in range(NT):
                link(dve.scalar_tensor_tensor(out=work[:, t], in0=xs[:, t], scalar=mv[:, 2, t, 0:1], in1=scores[:, t],
                                              op0=ALU.subtract, op1=ALU.mult))
                link(dve.tensor_tensor_reduce(out=work[:, t], in0=work[:, t], in1=pen[:, t], scale=1.0, scalar=2 * MASKED,
                                              op0=ALU.add, op1=ALU.max, accum_out=row_max[:, t:t + 1]))
                dve.scalar_tensor_tensor(out=exp_bias[:, t:t + 1], in0=row_max[:, t:t + 1], scalar=-1.0,
                                         in1=rstd[:, 2, t:t + 1], op0=ALU.mult, op1=ALU.mult).then_inc(ebias_ready, 1)
            link(dve.tensor_scalar(live[:], row_max[:], MASKED / 2, None, ALU.is_gt))
            dve.wait_ge(exp_ready, NT)
            link(dve.tensor_tensor(row_sum[:], row_sum[:], live[:], ALU.mult))
            link(dve.reciprocal(inv_sum[:], row_sum[:]))
            link(dve.scalar_tensor_tensor(out=inv_sum[:], in0=inv_sum[:], scalar=tg[:, 1:2], in1=live[:], op0=ALU.mult, op1=ALU.mult))
            for t in range(NT):
                last = dve.scalar_tensor_tensor(out=xs[:, t], in0=work[:, t], scalar=inv_sum[:, t:t + 1], in1=xs[:, t],
                                                op0=ALU.mult, op1=ALU.add)
            link(last)
            dve.sem_inc(x3_ready, 1)
            statistics(3)
            dve.wait_ge(var_ready, 4 * NT)
            normalise(3)
            evacuate_xnt(F_XNT2, False)
            emptied(dve, F_LOGIT[B - 1])
            for t in range(NT):
                last = dve.max(l_max[:, t], e_rest[:, t])
            link(last)
            dve.tensor_scalar(l_neg[:], l_max[:, :, 0], -1.0, None, ALU.mult).then_inc(l_neg_ready, 1)
            for t in range(NT):
                dve.wait_ge(e_ready, t + 1)
                link(dve.max(e_top[:, t], e_val[:, t]))
                link(dve.match_replace(e_rest[:, t], e_top[:, t], e_val[:, t], -1.0))
                dve.tensor_scalar(chosen[:, t], e_rest[:, t], 0.0, None, ALU.is_lt)
                link(dve.scalar_tensor_tensor(out=e_rest[:, t], in0=e_rest[:, t], scalar=0.0, in1=e_val[:, t], op0=ALU.is_lt,
                                              op1=ALU.mult, accum_out=l_neg[:, t:t + 1]))
                link(dve.reciprocal(l_max[:, t, 0:1], l_neg[:, t:t + 1]))
                link(dve.tensor_scalar(rw[:, t], e_rest[:, t], l_max[:, t, 0:1], tg[:, 3:4], ALU.mult, ALU.mult))
            dve.sem_inc(chosen_ready, 1)
            link(dve.tensor_scalar(rw[:], rw[:], W_SCALE, None, ALU.mult))
            link(dve.tensor_copy(w_parts[:, :, :, 0], rw[:]))
            link(dve.tensor_tensor(w_rest[:], rw[:], w_parts[:, :, :, 0], ALU.subtract))
            link(dve.tensor_copy(w_parts[:, :, :, 1], w_rest[:]))
            link(dve.tensor_tensor(w_rest[:], w_rest[:], w_parts[:, :, :, 1], ALU.subtract))
            link(dve.tensor_copy(w_parts[:, :, :, 2], w_rest[:]))
            filled(F_RANK)
            link(dve.scalar_tensor_tensor(out=rank[:].rearrange("p t e -> p (t e)"), in0=bank(F_RANK), scalar=1.0,
                                          in1=chosen[:].rearrange("p t e -> p (t e)"), op0=ALU.add, op1=ALU.mult))
            dve.tensor_scalar(rank[:], rank[:], -1.0, None, ALU.add).then_inc(dve_evac, 1)
            filled(F_COUNT)
            dve.tensor_scalar(n_tiles_i[:, 0], bank(F_COUNT)[:, 0:NE], float(P - 1), None, ALU.add).then_inc(dve_evac, 1)
            emptied(dve, F_COUNT)
            link(dve.tensor_scalar(n_tiles_i[:, 1], n_tiles_i[:, 0], 7, None, ALU.arith_shift_right))
            link(dve.tensor_copy(n_tiles[:], n_tiles_i[:, 1]))
            link(dve.memset(list_scratch[:], 0.0))
            link(dve.tensor_tensor_scan(tiles_end[:], n_tiles[:], list_scratch[:, 0], 0.0, ALU.add, ALU.add))
            dve.wait_ge(consts_ready, 7)
            link(dve.tensor_scalar(list_scratch[:, 0], tiles_end[:], row_id[:], 0.0, ALU.is_le, ALU.add, accum_out=tile_of[:, 0:1]))
            link(dve.scalar_tensor_tensor(out=list_scratch[:, 1], in0=tiles_end[:], scalar=row_id[:], in1=n_tiles[:],
                                          op0=ALU.is_le, op1=ALU.mult, accum_out=tile_of[:, 1:2]))
            link(dve.tensor_tensor(tile_of[:, 1:2], row_id[:], tile_of[:, 1:2], ALU.subtract))
            link(dve.tensor_scalar(tile_of[:, 2:3], tile_of[:, 0:1], float(NE), float(MAX_COUNT_TILES), ALU.is_ge, ALU.mult))
            link(dve.tensor_tensor(tile_of[:, 1:2], tile_of[:, 1:2], tile_of[:, 2:3], ALU.add))
            link(dve.tensor_scalar(tile_of[:, 0:1], tile_of[:, 0:1], float(NE - 1), None, ALU.min))
            link(dve.tensor_scalar(tile_of[:, 1:2], tile_of[:, 1:2], float(P), None, ALU.mult))
            for n in range(2):
                last = dve.tensor_scalar(tile_diag[:, n], ident[:], tile_of[:, n:n + 1], None, ALU.mult)
            last.then_inc(diag_ready, 1)
            link(dve.tensor_scalar(n_tiles_i[0:1, 0, 0:1], tiles_end[0:1, NE - 1:NE], float(LANES - 1), None, ALU.add))
            link(dve.tensor_scalar(n_tiles_i[0:1, 1, 0:1], n_tiles_i[0:1, 0, 0:1], 2, None, ALU.arith_shift_right))
            link(dve.tensor_scalar(n_quads[0:1, 0:1], n_tiles_i[0:1, 1, 0:1], 2.0, None, ALU.subtract))
            filled(F_TILES)
            dve.tensor_copy(first_rank[:], bank(F_TILES)[:, P:2 * P])
            dve.tensor_copy(expert_of[:], bank(F_TILES)[0:1, 0:P]).then_inc(dve_evac, 1)
            emptied(dve, F_TILES)
            dve.sem_inc(lists_ready, 1)

            def load_expert(tile):
                return dve.value_load(expert_of[0:1, bass.ds(tile.j, 1)], min_val=0, max_val=NE - 1)

            def prepare(tile, e):
                need(dve, list_filled, tile.j - 1)
                two = tile.two
                dve.tensor_tensor(local[:, two], rank[:, :, bass.ds(e, 1)].rearrange("p t a -> p (t a)"),
                                  first_rank[:, bass.ds(tile.j, 1)].to_broadcast([P, NT]), ALU.subtract).then_inc(local_ready, 1)
                dve.wait_ge(local_ready, tile.j + 1)
                dve.tensor_tensor(cols[:, two, :, 0], token_id[:], local[:, two], ALU.subtract)
                dve.tensor_copy(cols[:, two, :, 1:N_COLS], w_parts[:, :, bass.ds(e, 1), :].rearrange("p t a n -> p t (a n)"))
                dve.tensor_tensor(one_hot[:, two], slot_id[:], local[:, two].rearrange("p (t a) -> p t a", a=1).to_broadcast([P, NT, P]),
                                  ALU.is_equal).then_inc(cols_ready, 1)

            def slot(tile, left):
                e = load_expert(tile.later(4)) if left is None else None
                dve.wait_ge(silu1_ready, tile.j + 1)
                need(dve, y_filled, tile.j - 1)
                dve.tensor_tensor(h1_t[:, tile.two], silu1[:, tile.two], psum[0:I1, 4 + tile.two, P:2 * P], ALU.mult).then_inc(h_ready, 1)
                if left is None:
                    prepare(tile.later(4), e)

            for n in range(LANES):
                prepare(Tile(0, n), load_expert(Tile(0, n)))
            over_tiles(dve, slot)
            dve.wait_ge(sums_loaded, 16 * N_SUMS)
            link(dve.tensor_tensor(xs[:], base[:], adj[:], ALU.add))
            link(dve.tensor_tensor(sim[:], sim[:], work[:], ALU.add))
            dve.tensor_tensor(xs[:], xs[:], sim[:], ALU.add).then_inc(out_ready, 1)


_INS = ["x", "ctx_512", "mask_SxS2_bk1", "mask_BxS2_bf0", "g_xattn", "g_ffn", "L0_xattn_Wq", "L0_xattn_Wk",
        "L0_xattn_gamma_raw", "L0_ffn_gate_up_proj", "L0_ffn_down_proj", "L1_xattn_Wq", "L1_xattn_bq", "L1_xattn_Wk",
        "L1_xattn_bk", "L1_ffn_gate_w", "L1_ffn_w_gate", "L1_ffn_w_up", "L1_ffn_w_down"]


def kernel(**inputs):
    import numpy as _np
    import concourse.bacc as _bacc
    from concourse import mybir as _mybir
    from concourse.bass_utils import run_bass_kernel_spmd as _run

    nc = _bacc.Bacc("TRN2", target_bir_lowering=False, num_devices=1)
    arrays, args = {}, []
    for name in _INS:
        a = _np.ascontiguousarray(inputs[name])
        if a.ndim == 0:
            a = a.reshape(1, 1)
        arrays[f"in_{name}"] = a
        args.append(nc.dram_tensor(f"in_{name}", a.shape, _mybir.dt.from_np(a.dtype), kind="ExternalInput").ap())
    x = arrays["in_x"]
    out = nc.dram_tensor("out_0", x.shape, _mybir.dt.from_np(x.dtype), kind="ExternalOutput").ap()
    gated_layers_kernel(nc, *args, out)
    r = _run(nc, [arrays], core_ids=[0])
    return r.results[0]["out_0"]
```

```python
from contextlib import ExitStack

import concourse.bass as bass
from concourse import mybir

F32 = mybir.dt.float32
U8 = mybir.dt.uint8
BF16 = mybir.dt.bfloat16
F16 = mybir.dt.float16
I32 = mybir.dt.int32
U32 = mybir.dt.uint32
ALU = mybir.AluOpType
ACT = mybir.ActivationFunctionType

P = 128
EPS = 1e-5
TOP_K_RATIO = 0.3
HEADS0 = 4
TOP_K_EXPERTS = 8
MASKED = -1e35
FLOOR = -1e30
REMOVED = -3e38
N_BANKS = 8
BANK = 512
LANES = 4
PARTS = 3
W_SCALE = 4096.0
N_COLS = 1 + PARTS
FIRST_QUADS = 2
LAST_QUADS = 2
AHEAD = 5
N_SUMS = 2


def gated_layers_kernel(nc, x, ctx_in, mask_ss, mask_bs, g_xattn, g_ffn, wq0, wk0, gamma_raw, gate_up, down,
                        wq1, bq1, wk1, bk1, router_w, w_gate, w_up, w_down, out):
    B, S, D = x.shape
    C = ctx_in.shape[2]
    NT = B * S // P
    HB = S // P
    NE0, _, GU = gate_up.shape
    I0 = GU // 2
    KC = D // P
    IC = I0 // P
    T = B * S
    NE, _, I1 = w_gate.shape
    HALF = T // 2
    TE = HALF // NE0
    TOPK = max(1, int(S * TOP_K_RATIO))
    ROUNDS = -(-TOPK // 8)
    SIM_SCALE = 1.0 / (float(C // HEADS0) ** 0.5 * HEADS0)
    SCORE_SCALE = float(C) ** -0.5

    x_f = x.rearrange("b s d -> (b s) d").rearrange("(t p) d -> p t d", p=P)
    out_f = out.rearrange("b s d -> (b s) d").rearrange("(t p) d -> p t d", p=P)
    ctx_f = ctx_in.rearrange("b s d -> (b s) d").rearrange("(t p) d -> p t d", p=P)
    MIN_QUADS = T * TOP_K_EXPERTS // P // LANES
    MAX_QUADS = P // LANES
    MAX_COUNT_TILES = T // P
    xn_dram = nc.dram_tensor("normed_rows", [T + P, D], F32, kind="Internal").ap()
    sums_dram = [nc.dram_tensor(f"expert_sums{n}", [T + P, D], F32, kind="Internal").ap() for n in range(N_SUMS)]

    with ExitStack() as stack:
        def sb(name, shape, dt=F32):
            return stack.enter_context(nc.sbuf_tensor(name, shape, dt))

        def sem(name):
            return stack.enter_context(nc.semaphore(name))

        ident = sb("ident", [P, P])
        xs = sb("xs", [P, NT, D])
        ctx_rows = sb("ctx_rows", [P, NT, C])
        ctx_t = sb("ctx_t", [C, T])
        w_rows = sb("w_rows", [C, 4, C])
        w_t = sb("w_t", [C, 4, C])
        bias1 = sb("bias1", [C, 2])
        proj_t = sb("proj_t", [C, 4, T])
        sim = sb("sim", [P, NT, S])
        work = sb("work", [P, NT, S])
        top8 = sb("top8", [P, NT, ROUNDS, 8])
        adj = sb("adj", [P, NT, S])
        scores = sb("scores", [P, NT, S])
        x3 = scores
        mask_s8 = sb("mask_s8", [P, HB, S], U8)
        mask_b8 = sb("mask_b8", [P, B, S], U8)
        pen_s = sb("pen_s", [P, HB, S])
        pen_b = sb("pen_b", [P, B, S])
        pen = sb("pen", [P, NT, S])
        gates = sb("gates", [P, 5])
        tg = sb("tg", [P, 4])
        gam = sb("gam", [P, 1])
        coef = sb("coef", [P, 4])
        stats = sb("stats", [P, NT, 6])
        mv = sb("mv", [P, 4, NT, 2])
        rstd = sb("rstd", [P, 4, NT])
        var_eps = sb("var_eps", [P, 4, NT])
        minus_half = sb("minus_half", [P, NT])
        neg_mean = sb("neg_mean", [P, 4, NT])
        shift = sb("shift", [P, 4, NT])
        a_scale = sb("a_scale", [P, NT])
        a_shift = sb("a_shift", [P, NT])
        base = sb("base", [P, NT, D])
        xn = sb("xn", [P, NT, D])
        xn_t = sb("xn_t", [P, KC, T])
        gu_w = sb("gu_w", [P, NE0, KC, GU])
        down_w = sb("down_w", [P, NE0, IC, D])
        silu0 = sb("silu0", [P, 2, IC * TE])
        up0 = sb("up0", [P, 2, IC * TE])
        h0_t = sb("h0_t", [P, 2, IC, TE])
        y0_t = sb("y0_t", [P, KC, T])
        row_max = sb("row_max", [P, NT])
        exp_bias = sb("exp_bias", [P, NT])
        row_sum = sb("row_sum", [P, NT])
        inv_sum = sb("inv_sum", [P, NT])
        live = sb("live", [P, NT])
        dead_nan = sb("dead_nan", [P, NT])
        router = sb("router", [P, KC, NE])
        logits = sb("logits", [P, NT, NE])
        logits_left = sb("logits_left", [P, NT, NE])
        l_top = sb("l_top", [P, NT, TOP_K_EXPERTS])
        l_neg = sb("l_neg", [P, NT])
        e_val = sb("e_val", [P, NT, NE])
        e_sum = sb("e_sum", [P, NT])
        e_scale = sb("e_scale", [P, NT])
        rw = sb("rw", [P, NT, NE])
        zeros = sb("zeros", [P, 2 * BANK])
        chosen = sb("chosen", [P, NT, NE], BF16)
        before = sb("before", [P, P], BF16)
        ones_b = sb("ones_b", [P, P], BF16)
        ones_f = sb("ones_f", [P, P])
        rank = sb("rank", [P, NT, NE])
        w_rest = sb("w_rest", [P, PARTS - 1, NT, NE])
        w_parts = sb("w_parts", [P, NT, NE, PARTS], F16)
        n_tiles = sb("n_tiles", [P, NE])
        n_tiles_i = sb("n_tiles_i", [P, 2, NE], I32)
        tiles_end = sb("tiles_end", [P, NE])
        list_scratch = sb("list_scratch", [P, 2, NE])
        row_id = sb("row_id", [P, 1])
        empty_row = sb("empty_row", [P, 1])
        token_id = sb("token_id", [P, NT])
        slot_id = sb("slot_id", [P, P, NT], F16)
        tile_of = sb("tile_of", [P, 4])
        tile_diag = sb("tile_diag", [P, 2, P])
        first_rank = sb("first_rank", [P, P])
        expert_of = sb("expert_of", [1, P], I32)
        n_quads = sb("n_quads", [1, 1], I32)
        local = sb("local", [P, 2, NT], F16)
        one_hot = sb("one_hot", [P, 2, P, NT], F16)
        cols = sb("cols", [P, 2, NT, N_COLS], F16)
        w_seen = sb("w_seen", [P, 2, PARTS])
        slot_w = sb("slot_w", [P, P])
        gather_at = sb("gather_at", [P, LANES], U32)
        scatter_at = sb("scatter_at", [P, LANES], U32)
        x_slots = sb("x_slots", [P, LANES, D])
        x_slots_t = sb("x_slots_t", [P, 2, KC, P])
        wg = sb("wg", [P, LANES, KC, I1])
        wu = sb("wu", [P, LANES, KC, I1])
        wd = sb("wd", [I1, LANES, D])
        silu1 = sb("silu1", [I1, 2, P])
        h1_t = sb("h1_t", [I1, 2, P])
        y_slots = sb("y_slots", [P, LANES, D])
        psum = stack.enter_context(nc.psum_tensor("psum", [P, N_BANKS, BANK], F32))

        ld = {n: sem("ld_" + n) for n in ("x", "ctx", "w", "bias", "gates", "ms", "mb", "gu", "down", "router")}
        ident_zero, ident_ready = sem("ident_zero"), sem("ident_ready")
        bank_filled = sem("bank_filled")
        evac = {who: sem(who + "_evac") for who in ("act", "dve")}
        tanh_ready = sem("tanh_ready")
        coef_ready = sem("coef_ready")
        dve_step = sem("dve_step")
        pen_step, pen_ready = sem("pen_step"), sem("pen_ready")
        sig_ready, adj_ready = sem("sig_ready"), sem("adj_ready")
        base_ready = sem("base_ready")
        var_ready, rstd_ready, shift_ready = sem("var_ready"), sem("rstd_ready"), sem("shift_ready")
        top8_ready, rest_ready = sem("top8_ready"), sem("rest_ready")
        ab_ready = sem("ab_ready")
        xn_ready = sem("xn_ready")
        h0_ready = sem("h0_ready")
        ebias_ready, exp_ready, dead_ready = sem("ebias_ready"), sem("exp_ready"), sem("dead_ready")
        l_neg_ready, e_ready, rw_ready = sem("l_neg_ready"), sem("e_ready"), sem("rw_ready")
        part_ready, rest_w_ready = sem("part_ready"), sem("rest_w_ready")
        zeros_ready, consts_ready = sem("zeros_ready"), sem("consts_ready")
        scratch_zeroed, x3_ready, x3_stored, xn_stored = sem("scratch_zeroed"), sem("x3_ready"), sem("x3_stored"), sem("xn_stored")
        chosen_ready, diag_ready, lists_ready = sem("chosen_ready"), sem("diag_ready"), sem("lists_ready")
        cols_ready, list_filled, list_copied = sem("cols_ready"), sem("list_filled"), sem("list_copied")
        gathered = [sem(f"gathered{n}") for n in range(LANES)]
        w_landed = [sem(f"w_landed{n}") for n in range(LANES)]
        scattered = [sem(f"scattered{n}") for n in range(N_SUMS)]
        xt_filled, xt_copied, gu_filled = sem("xt_filled"), sem("xt_copied"), sem("gu_filled")
        silu1_ready, h_ready, y_filled, y_ready = sem("silu1_ready"), sem("h_ready"), sem("y_filled"), sem("y_ready")
        local_ready, rows_kept = sem("local_ready"), sem("rows_kept")
        gathers_begun, scatters_begun, weighing = sem("gathers_begun"), sem("scatters_begun"), sem("weighing")
        sums_loaded = [sem(f"sums_loaded{c}") for c in range(B)]
        out_ready, stored = sem("out_ready"), sem("stored")

        fills = []

        def add_fill(name, engine):
            fills.append((name, engine))
            return len(fills) - 1

        F_CTX, F_PROJ, F_SIM, F_SCORE = {}, {}, {}, {}
        F_CTX[0] = add_fill("ctx", "act")
        F_W = add_fill("w", "dve")
        F_PROJ[0, 0], F_PROJ[1, 0] = add_fill("q0", "act"), add_fill("k0", "dve")
        F_SIM[0], F_SIM[1] = add_fill("sim", "dve"), add_fill("sim", "act")
        F_CTX[1] = add_fill("ctx", "act")
        F_PROJ[0, 1], F_PROJ[1, 1] = add_fill("q0", "act"), add_fill("k0", "act")
        F_SIM[2], F_SIM[3] = add_fill("sim", "act"), add_fill("sim", "act")
        for w in (2, 3):
            for half in range(2):
                F_PROJ[w, half] = add_fill("proj", "act")
        for b in range(B):
            F_SCORE[b] = add_fill("score", "act")

        F_ADJT, F_XNT, F_YT, F_XNT2, F_LOGIT = {}, {}, {}, {}, {}
        F_GATE, F_UP, F_DOWN = {}, {}, {}

        def add_gate_up_fills(q):
            F_GATE[q], F_UP[q] = add_fill("gate", "act"), add_fill("up", "act")

        def add_down_fill(q):
            F_DOWN[q] = add_fill("down", "act")

        for fill, name, who in ((F_ADJT, "adjt", "dve"), (F_XNT, "xnt", "act")):
            for b in (0, 1):
                fill[b] = add_fill(name, who)
        for q in range(NE0):
            if q == NE0 - 1:
                F_ADJT[2] = add_fill("adjt", "dve")
            add_gate_up_fills(q)
            if q:
                add_down_fill(q - 1)
        add_down_fill(NE0 - 1)
        F_XNT[2] = add_fill("xnt", "act")
        F_ADJT[3] = add_fill("adjt", "dve")
        F_YT[0], F_YT[1] = add_fill("yt", "dve"), add_fill("yt", "dve")
        F_XNT[3] = add_fill("xnt", "act")
        add_gate_up_fills(NE0)
        for q in range(NE0 + 1, 2 * NE0 - 1):
            add_gate_up_fills(q)
            add_down_fill(q - 1)
        F_XNT2[0], F_XNT2[1] = add_fill("xnt2", "act"), add_fill("xnt2", "act")
        add_gate_up_fills(2 * NE0 - 1)
        F_LOGIT[0], F_LOGIT[1] = add_fill("logit", "act"), add_fill("logit", "act")
        add_down_fill(2 * NE0 - 2)
        add_down_fill(2 * NE0 - 1)
        F_YT[2], F_YT[3] = add_fill("yt", "dve"), add_fill("yt", "dve")
        for b in (2, 3):
            F_XNT2[b] = add_fill("xnt2", "act")
            F_LOGIT[b] = add_fill("logit", "act")
        F_COUNT = add_fill("count", "dve")
        F_RANK = add_fill("rank", "dve")
        F_TILES = add_fill("tiles", "dve")

        def emptied(eng, i):
            who = fills[i][1]
            n = sum(1 for f in fills[:i + 1] if f[1] == who)
            eng.wait_ge(evac[who], n)

        def bank(i):
            return psum[:, i % N_BANKS, :]

        LAYERNORMS = ((0, None), (1, 0), (1, 1), (1, 2), (1, 3), (2, 0), (2, 1), (3, 0), (3, 1), (2, 2), (2, 3), (3, 2), (3, 3))

        def layernorm_count(n, b):
            return LAYERNORMS.index((n, b)) + 1

        def tiles_of(b):
            return range(0, NT) if b is None else range(b * HB, (b + 1) * HB)

        def span(b):
            return slice(tiles_of(b).start, tiles_of(b).stop)

        def xn_t_view(k, b, permuted):
            if permuted:
                return xn_t[:, k].rearrange("p (f e b g) -> p f e b g", f=2, e=NE0, b=B // 2)[:, b // 2, :, b % 2, :]
            return xn_t[:, k, b * S:(b + 1) * S]

        def xn_bank_view(i, k, permuted):
            src = bank(i)[:, k * S:(k + 1) * S]
            return src.rearrange("p (g e) -> p e g", e=NE0) if permuted else src

        def need(eng, semaphore, n):
            if not (isinstance(n, int) and n <= 0):
                eng.wait_ge(semaphore, n)

        class Tile:

            def __init__(self, quad, lane):
                self.quad, self.lane = quad, lane
                self.j = quad * LANES + lane
                self.two = lane % 2

            def later(self, n):
                return Tile(self.quad + (self.lane + n) // LANES, (self.lane + n) % LANES)

            def sum(self):
                return self.lane % N_SUMS, self.quad * (LANES // N_SUMS) + self.lane // N_SUMS

            def before(self):
                return self.later(-1)

        def over_tiles(eng, slot):
            eng.wait_ge(lists_ready, 1)
            inner_quads = eng.value_load(n_quads[0:1, 0:1], min_val=MIN_QUADS - FIRST_QUADS - LAST_QUADS,
                                         max_val=MAX_QUADS - FIRST_QUADS - LAST_QUADS)
            for quad in range(FIRST_QUADS):
                for lane in range(LANES):
                    slot(Tile(quad, lane), None)
            with eng.Fori(FIRST_QUADS, inner_quads + FIRST_QUADS) as quad:
                for lane in range(LANES):
                    slot(Tile(quad, lane), None)
            for n in range(LAST_QUADS * LANES):
                slot(Tile(inner_quads + FIRST_QUADS, 0).later(n), LAST_QUADS * LANES - 1 - n)
            return Tile(inner_quads + FIRST_QUADS + LAST_QUADS - 1, LANES - 1)

        def follows(left, n):
            return left is None or left >= n

        def first(tile):
            return isinstance(tile.j, int) and tile.j == 0

        block = stack.enter_context(nc.Block())

        @block.sync
        def _(sp):
            sp.dma_start(ctx_rows[:], ctx_f).then_inc(ld["ctx"], 16)
            for i, w in enumerate((wq0, wk0, wq1, wk1)):
                sp.dma_start(w_rows[:, i, :], w).then_inc(ld["w"], 16)
            sp.dma_start(bias1[:, 0:1], bq1.rearrange("(c a) -> c a", a=1)).then_inc(ld["bias"], 16)
            sp.dma_start(bias1[:, 1:2], bk1.rearrange("(c a) -> c a", a=1)).then_inc(ld["bias"], 16)
            sp.dma_start(xs[:], x_f).then_inc(ld["x"], 16)
            sp.dma_start(gates[:, 0:2], g_xattn.rearrange("(a n) -> a n", a=1).to_broadcast([P, 2])).then_inc(ld["gates"], 16)
            sp.dma_start(gates[:, 2:4], g_ffn.rearrange("(a n) -> a n", a=1).to_broadcast([P, 2])).then_inc(ld["gates"], 16)
            sp.dma_start(gates[:, 4:5], gamma_raw.to_broadcast([P, 1])).then_inc(ld["gates"], 16)
            sp.dma_start(mask_s8[:], mask_ss.rearrange("(h p) m -> p h m", p=P)).then_inc(ld["ms"], 16)
            sp.dma_start(mask_b8[:].rearrange("p b s -> p (b s)"), mask_bs.rearrange("(a b) s -> a (b s)", a=1).to_broadcast([P, B * S])).then_inc(ld["mb"], 16)
            for e in range(NE0):
                sp.dma_start(gu_w[:, e], gate_up[e].rearrange("(k p) n -> p k n", p=P)).then_inc(ld["gu"], 16)
            for e in range(NE0):
                sp.dma_start(down_w[:, e], down[e].rearrange("(k p) n -> p k n", p=P)).then_inc(ld["down"], 16)
            sp.dma_start(router[:], router_w.rearrange("(k p) n -> p k n", p=P)).then_inc(ld["router"], 16)
            sp.wait_ge(zeros_ready, 1)
            z_rows = zeros[:, 0:2 * BANK].rearrange("p (r d) -> p r d", d=D)
            for rows in sums_dram[1:]:
                for n in range(NT // 4):
                    sp.dma_start(rows[n * 4 * P:(n + 1) * 4 * P, :].rearrange("(p r) d -> p r d", p=P), z_rows).then_inc(scratch_zeroed, 16)
            for rows in (*sums_dram, xn_dram):
                sp.dma_start(rows[T:T + P, :], zeros[:, 0:D]).then_inc(scratch_zeroed, 16)
            sp.wait_ge(x3_ready, NT)
            sp.dma_start(sums_dram[0][0:T, :].rearrange("(t p) d -> p t d", p=P), x3[:]).then_inc(x3_stored, 16)
            sp.wait_ge(xn_ready, 2 * NT)
            sp.dma_start(xn_dram[0:T, :].rearrange("(t p) d -> p t d", p=P), xn[:]).then_inc(xn_stored, 16)

            quad_experts = []

            def load_weights(tile, left):
                if tile.lane == 0:
                    _, quad_experts[:] = nc.values_load_multi_w_load_instructions(
                        expert_of[0:1, bass.ds(tile.j, LANES)], engines=[mybir.EngineType.SP], min_val=0, max_val=NE - 1)
                e = quad_experts[tile.lane]
                need(sp, y_filled, tile.j - LANES + 1)
                n = tile.lane
                sp.dma_start(wg[:, n], w_gate[bass.ds(e, 1)].rearrange("a (p k) n -> p (a k) n", p=P)).then_inc(w_landed[n], 16)
                sp.dma_start(wu[:, n], w_up[bass.ds(e, 1)].rearrange("a (p k) n -> p (a k) n", p=P)).then_inc(w_landed[n], 16)
                sp.dma_start(wd[:, n], w_down[bass.ds(e, 1)].rearrange("a p n -> p (a n)")).then_inc(w_landed[n], 16)

            last_quad = over_tiles(sp, load_weights).quad
            for n in range(N_SUMS):
                sp.wait_ge(scattered[n], last_quad * (16 * LANES // N_SUMS) + 16 * LANES // N_SUMS)
                for c in range(B):
                    sp.dma_start((base, adj)[n][:, span(c)], sums_dram[n][c * S:(c + 1) * S, :].rearrange("(t p) d -> p t d", p=P)).then_inc(sums_loaded[c], 16)
            for c in range(B):
                sp.wait_ge(out_ready, c + 1)
                sp.dma_start(out_f[:, c * HB:(c + 1) * HB], xs[:, c * HB:(c + 1) * HB]).then_inc(stored, 16)
            sp.wait_ge(stored, 16 * B)

        @block.gpsimd
        def _(pool):
            pool.memset(ident[:], 0.0).then_inc(ident_zero, 1)
            pool.wait_ge(ident_zero, 1)
            pool.affine_select(out=ident[:], in_=ident[:], compare_op=ALU.not_equal, fill=1.0, base=0,
                               pattern=[[-1, P]], channel_multiplier=1).then_inc(ident_ready, 1)
            pool.memset(zeros[:], 0.0).then_inc(zeros_ready, 1)
            pool.memset(minus_half[:], -0.5).then_inc(pen_step, 1)
            pool.memset(ones_b[:], 1.0).then_inc(consts_ready, 1)
            pool.memset(ones_f[:], 1.0).then_inc(consts_ready, 1)
            pool.iota(row_id[:], [[0, 1]], base=0, channel_multiplier=1, allow_small_or_imprecise_dtypes=True).then_inc(consts_ready, 1)
            pool.iota(empty_row[:], [[0, 1]], base=T, channel_multiplier=1, allow_small_or_imprecise_dtypes=True).then_inc(consts_ready, 1)
            pool.iota(slot_id[:], [[1, P], [0, NT]], base=0, channel_multiplier=0, allow_small_or_imprecise_dtypes=True).then_inc(consts_ready, 1)
            pool.iota(token_id[:], [[P, NT]], base=-T, channel_multiplier=1, allow_small_or_imprecise_dtypes=True).then_inc(consts_ready, 1)
            pool.wait_ge(consts_ready, 6)
            pool.affine_select(out=before[:], in_=ones_b[:], compare_op=ALU.is_gt, fill=0.0, base=0,
                               pattern=[[1, P]], channel_multiplier=-1).then_inc(consts_ready, 1)
            pool.wait_ge(ld["ms"], 16)
            pool.tensor_scalar(pen_s[:], mask_s8[:], MASKED, None, ALU.mult).then_inc(pen_step, 1)
            pool.wait_ge(ld["mb"], 16)
            pool.tensor_scalar(pen_b[:], mask_b8[:], MASKED, None, ALU.mult).then_inc(pen_step, 1)
            pool.wait_ge(pen_step, 3)

            for b in range(B):
                for h in range(HB):
                    pool.tensor_tensor(pen[:, b * HB + h], pen_s[:, h], pen_b[:, b], ALU.add).then_inc(pen_ready, 1)

            def inverse_deviation(n, b):
                tiles, count = span(b), layernorm_count(n, b)
                pool.wait_ge(var_ready, count)
                pool.tensor_tensor(rstd[:, n, tiles], var_eps[:, n, tiles], minus_half[:, tiles], ALU.pow).then_inc(rstd_ready, 1)
                pool.wait_ge(rstd_ready, count)
                pool.tensor_tensor(shift[:, n, tiles], neg_mean[:, n, tiles], rstd[:, n, tiles], ALU.mult).then_inc(shift_ready, 1)

            def up_times_silu(half, experts):
                for e in experts:
                    q = half * NE0 + e
                    emptied(pool, F_UP[q])
                    if q >= 2:
                        pool.wait_ge(bank_filled, F_DOWN[q - 2] + 1)
                    pool.tensor_tensor(h0_t[:, q % 2].rearrange("p i t -> p (i t)"), silu0[:, q % 2], up0[:, q % 2],
                                       ALU.mult).then_inc(h0_ready, 1)

            inverse_deviation(0, None)
            pool.wait_ge(coef_ready, 1)
            pool.wait_ge(shift_ready, 1)
            pool.tensor_scalar(a_scale[:], rstd[:, 0], coef[:, 2:3], 1.0, ALU.mult, ALU.add).then_inc(ab_ready, 1)
            pool.tensor_scalar(a_shift[:], shift[:, 0], coef[:, 2:3], None, ALU.mult).then_inc(ab_ready, 1)
            inverse_deviation(1, 0)
            inverse_deviation(1, 1)
            up_times_silu(0, range(NE0))
            for n, b in ((1, 2), (1, 3), (2, 0), (2, 1)):
                inverse_deviation(n, b)
            up_times_silu(1, (0,))
            inverse_deviation(3, 0)
            up_times_silu(1, (1,))
            inverse_deviation(3, 1)
            up_times_silu(1, (2, 3))
            for n in (2, 3):
                for b in (2, 3):
                    inverse_deviation(n, b)
            for n in range(PARTS - 1):
                pool.wait_ge(part_ready, n + 1)
                pool.tensor_tensor(w_rest[:, n], w_rest[:, n - 1] if n else rw[:], w_parts[:, :, :, n], ALU.subtract).then_inc(rest_w_ready, 1)
            pool.wait_ge(scratch_zeroed, 16 * ((N_SUMS - 1) * NT // 4 + N_SUMS + 1))
            pool.wait_ge(x3_stored, 16)
            pool.wait_ge(xn_stored, 16)

            def gather(tile):
                need(pool, xt_filled, tile.j - LANES + 1)
                pool.wait_ge(list_copied, tile.j + 1)
                pool.sem_inc(gathers_begun, 1)
                pool.indirect_dma_start(x_slots[:, tile.lane, :], None, xn_dram,
                                        bass.IndirectOffsetOnAxis(ap=gather_at[:, tile.lane:tile.lane + 1], axis=0)).then_inc(gathered[tile.lane], 16)

            def scatter(tile):
                pool.wait_ge(y_ready, tile.j + 1)
                n, earlier = tile.sum()
                need(pool, scattered[n], earlier * 16)
                pool.sem_inc(scatters_begun, 1)
                pool.indirect_dma_start(sums_dram[n], bass.IndirectOffsetOnAxis(ap=scatter_at[:, tile.lane:tile.lane + 1], axis=0),
                                        y_slots[:, tile.lane, :], None, compute_op=ALU.add).then_inc(scattered[n], 16)

            def slot(tile, left):
                if not first(tile):
                    scatter(tile.before())
                if follows(left, AHEAD):
                    gather(tile.later(AHEAD))

            for n in range(AHEAD):
                gather(Tile(0, 0).later(n))
            scatter(over_tiles(pool, slot))

        @block.tensor
        def _(pe):
            def begin(i):
                if i >= N_BANKS:
                    emptied(pe, i - N_BANKS)

            pe.wait_ge(ident_ready, 1)
            def transpose_ctx(half):
                begin(F_CTX[half])
                for t in range(NT // 2):
                    last = pe.transpose(bank(F_CTX[half])[0:C, t * P:(t + 1) * P], ctx_rows[:, half * (NT // 2) + t, :], ident[:])
                last.then_inc(bank_filled, 1)

            def project(w, half):
                i = F_PROJ[w, half]
                begin(i)
                pe.matmul(bank(i)[0:C, :], w_t[:, w, :], ctx_t[:, half * HALF:(half + 1) * HALF], start=True, stop=True).then_inc(bank_filled, 1)

            def query_times_key(layer, fill, b):
                begin(fill[b])
                for h in range(HB):
                    t = b * HB + h
                    last = pe.matmul(bank(fill[b])[:, h * S:(h + 1) * S], proj_t[:, 2 * layer, t * P:(t + 1) * P],
                                     proj_t[:, 2 * layer + 1, b * S:(b + 1) * S], start=True, stop=True)
                last.then_inc(bank_filled, 1)

            pe.wait_ge(ld["ctx"], 16)
            transpose_ctx(0)
            pe.wait_ge(ld["w"], 64)
            begin(F_W)
            for i in range(4):
                last = pe.transpose(bank(F_W)[0:C, i * C:(i + 1) * C], w_rows[:, i, :], ident[0:C, 0:C])
            last.then_inc(bank_filled, 1)
            emptied(pe, F_W)
            for half in range(2):
                if half:
                    transpose_ctx(half)
                emptied(pe, F_CTX[half])
                for w in (0, 1):
                    project(w, half)
                for w in (0, 1):
                    emptied(pe, F_PROJ[w, half])
                for b in (2 * half, 2 * half + 1):
                    query_times_key(0, F_SIM, b)
            for w in (2, 3):
                for half in range(2):
                    project(w, half)
            for w in (2, 3):
                for half in range(2):
                    emptied(pe, F_PROJ[w, half])
            for b in range(B):
                query_times_key(1, F_SCORE, b)

            def transpose_adj(b):
                i = F_ADJT[b]
                begin(i)
                pe.wait_ge(adj_ready, HB * (b + 1))
                for h in range(HB):
                    for m in range(HB):
                        last = pe.transpose(bank(i)[:, h * S + m * P:h * S + (m + 1) * P],
                                            adj[:, b * HB + m, h * P:(h + 1) * P], ident[:])
                last.then_inc(bank_filled, 1)

            def transpose_normed(fill, ready, b):
                i = fill[b]
                begin(i)
                pe.wait_ge(xn_ready, ready + HB * (b + 1))
                for k in range(KC):
                    for h in range(HB):
                        last = pe.transpose(bank(i)[:, k * S + h * P:k * S + (h + 1) * P],
                                            xn[:, b * HB + h, k * P:(k + 1) * P], ident[:])
                last.then_inc(bank_filled, 1)

            def expert_down0(q):
                i = F_DOWN[q]
                begin(i)
                pe.wait_ge(h0_ready, q + 1)
                for hc in range(KC):
                    for ic in range(IC):
                        last = pe.matmul(bank(i)[:, hc * TE:(hc + 1) * TE], down_w[:, q % NE0, ic, hc * P:(hc + 1) * P],
                                         h0_t[:, q % 2, ic, :], start=ic == 0, stop=ic == IC - 1)
                last.then_inc(bank_filled, 1)

            def expert_gate_up0(q):
                half, e = q // NE0, q % NE0
                for part, fill in enumerate((F_GATE[q], F_UP[q])):
                    begin(fill)
                    for ic in range(IC):
                        for k in range(KC):
                            c = part * I0 + ic * P
                            last = pe.matmul(bank(fill)[:, ic * TE:(ic + 1) * TE], gu_w[:, e, k, c:c + P],
                                             xn_t[:, k, half * HALF + e * TE:half * HALF + (e + 1) * TE], start=k == 0, stop=k == KC - 1)
                    last.then_inc(bank_filled, 1)

            def transpose_y0(b):
                emptied(pe, F_DOWN[b // 2 * NE0 + NE0 - 1])
                i = F_YT[b]
                begin(i)
                for h in range(HB):
                    for k in range(KC):
                        t = b * HB + h
                        last = pe.transpose(bank(i)[:, h * D + k * P:h * D + (k + 1) * P],
                                            y0_t[:, k, t * P:(t + 1) * P], ident[:])
                last.then_inc(bank_filled, 1)

            def router_logits(b):
                i = F_LOGIT[b]
                emptied(pe, F_XNT2[b])
                begin(i)
                for h in range(HB):
                    t = b * HB + h
                    for k in range(KC):
                        last = pe.matmul(bank(i)[:, h * NE:(h + 1) * NE], xn_t[:, k, t * P:(t + 1) * P], router[:, k, :],
                                         start=k == 0, stop=k == KC - 1)
                last.then_inc(bank_filled, 1)

            transpose_adj(0)
            transpose_adj(1)
            transpose_normed(F_XNT, 0, 0)
            transpose_normed(F_XNT, 0, 1)
            pe.wait_ge(ld["gu"], 16 * NE0)
            pe.wait_ge(ld["down"], 16 * NE0)
            emptied(pe, F_XNT[1])
            for q in range(NE0):
                if q == NE0 - 1:
                    transpose_adj(2)
                expert_gate_up0(q)
                if q:
                    expert_down0(q - 1)
            expert_down0(NE0 - 1)
            transpose_normed(F_XNT, 0, 2)
            transpose_adj(3)
            transpose_y0(0)
            transpose_y0(1)
            transpose_normed(F_XNT, 0, 3)
            emptied(pe, F_XNT[3])
            expert_gate_up0(NE0)
            for q in range(NE0 + 1, 2 * NE0 - 1):
                expert_gate_up0(q)
                expert_down0(q - 1)
            transpose_normed(F_XNT2, NT, 0)
            transpose_normed(F_XNT2, NT, 1)
            expert_gate_up0(2 * NE0 - 1)
            pe.wait_ge(ld["router"], 16)
            router_logits(0)
            router_logits(1)
            expert_down0(2 * NE0 - 2)
            expert_down0(2 * NE0 - 1)
            transpose_y0(2)
            transpose_y0(3)
            for b in (2, 3):
                transpose_normed(F_XNT2, NT, b)
                router_logits(b)
            pe.wait_ge(chosen_ready, B)
            pe.wait_ge(consts_ready, 7)
            begin(F_COUNT)
            for t in range(NT):
                last = pe.matmul(bank(F_COUNT)[:, 0:NE], ones_b[:], chosen[:, t, :], start=t == 0, stop=t == NT - 1)
            last.then_inc(bank_filled, 1)
            begin(F_RANK)
            rank_ps = bank(F_RANK).rearrange("p (t e) -> p t e", t=NT)
            pe.matmul(rank_ps, before[:], chosen[:], start=True, stop=False)
            for t in range(NT - 1):
                last = pe.matmul(rank_ps[:, t + 1:NT, :], ones_b[:], chosen[:, t:t + 1, :].to_broadcast([P, NT - 1 - t, NE]),
                                 start=False, stop=t == NT - 2)
            last.then_inc(bank_filled, 1)
            begin(F_TILES)
            pe.wait_ge(diag_ready, 1)
            pe.matmul(bank(F_TILES)[:, 0:2 * P], ones_f[:], tile_diag[:].rearrange("p n j -> p (n j)"), start=True, stop=True).then_inc(bank_filled, 1)
            emptied(pe, F_TILES)
            emptied(pe, F_LOGIT[B - 1])

            def slot_lists(tile):
                pe.wait_ge(cols_ready, tile.j + 1)
                need(pe, list_copied, tile.j - 1)
                for t in range(NT):
                    last = pe.matmul(psum[:, tile.two, 0:N_COLS], one_hot[:, tile.two, :, t], cols[:, tile.two, t, :],
                                     start=t == 0, stop=t == NT - 1)
                last.then_inc(list_filled, 1)

            def transpose_slots(tile):
                pe.wait_ge(gathered[tile.lane], tile.quad * 16 + 16)
                need(pe, xt_copied, tile.j - 1)
                for k in range(KC):
                    last = pe.transpose(psum[:, 2 + tile.two, k * P:(k + 1) * P],
                                        x_slots[:, tile.lane, :].rearrange("p (n k) -> p k n", k=KC)[:, k, :], ident[:])
                last.then_inc(xt_filled, 1)

            def gate_up1(tile):
                pe.wait_ge(xt_copied, tile.j + 1)
                pe.wait_ge(w_landed[tile.lane], tile.quad * 48 + 48)
                need(pe, h_ready, tile.j - 1)
                for part, w in enumerate((wg, wu)):
                    for k in range(KC):
                        last = pe.matmul(psum[0:I1, 4 + tile.two, part * P:(part + 1) * P], w[:, tile.lane, k, :],
                                         x_slots_t[:, tile.two, k, :], start=k == 0, stop=k == KC - 1)
                last.then_inc(gu_filled, 1)

            def down1(tile):
                pe.wait_ge(h_ready, tile.j + 1)
                need(pe, y_ready, tile.j - 1)
                pe.matmul(psum[:, 6 + tile.two, 0:D], h1_t[:, tile.two, :], wd[:, tile.lane, :],
                          start=True, stop=True).then_inc(y_filled, 1)

            def slot(tile, left):
                gate_up1(tile)
                if not first(tile):
                    down1(tile.before())
                if follows(left, AHEAD):
                    slot_lists(tile.later(AHEAD))
                if follows(left, 2):
                    transpose_slots(tile.later(2))

            for n in range(LANES):
                slot_lists(Tile(0, n))
            transpose_slots(Tile(0, 0))
            slot_lists(Tile(1, 0))
            transpose_slots(Tile(0, 1))
            down1(over_tiles(pe, slot))

        @block.scalar
        def _(act):
            def filled(i):
                act.wait_ge(bank_filled, i + 1)

            def copy_ctx(half):
                filled(F_CTX[half])
                act.copy(ctx_t[:, half * HALF:(half + 1) * HALF], bank(F_CTX[half])[0:C, :]).then_inc(evac["act"], 1)

            def copy_projection(w, half):
                i = F_PROJ[w, half]
                filled(i)
                dst = proj_t[:, w, half * HALF:(half + 1) * HALF]
                if w < 2:
                    act.copy(dst, bank(i)[0:C, :]).then_inc(evac["act"], 1)
                else:
                    act.activation(dst, bank(i)[0:C, :], ACT.Identity, bias=bias1[:, w - 2:w - 1]).then_inc(evac["act"], 1)

            def copy_scaled(dst, fill, b, scale):
                filled(fill[b])
                act.mul(dst[:, span(b)].rearrange("p h s -> p (h s)"), bank(fill[b]), scale).then_inc(evac["act"], 1)

            copy_ctx(0)
            copy_projection(0, 0)
            copy_scaled(sim, F_SIM, 1, SIM_SCALE)
            copy_ctx(1)
            copy_projection(0, 1)
            copy_projection(1, 1)
            copy_scaled(sim, F_SIM, 2, SIM_SCALE)
            copy_scaled(sim, F_SIM, 3, SIM_SCALE)
            act.wait_ge(ld["gates"], 48)
            act.activation(tg[:], gates[:, 0:4], ACT.Tanh).then_inc(tanh_ready, 1)
            act.activation(gam[:], gates[:, 4:5], ACT.Sigmoid).then_inc(tanh_ready, 1)
            for b in range(B):
                emptied(act, F_SIM[b])
                act.activation(adj[:, span(b)], sim[:, span(b)], ACT.Sigmoid).then_inc(sig_ready, 1)
            act.wait_ge(ld["bias"], 32)
            for w in (2, 3):
                for half in range(2):
                    copy_projection(w, half)
            for b in range(B):
                copy_scaled(scores, F_SCORE, b, SCORE_SCALE)
            act.wait_ge(ab_ready, 2)
            for t in range(NT):
                act.activation(base[:, t], xs[:, t], ACT.Identity, bias=a_shift[:, t:t + 1], scale=a_scale[:, t:t + 1]).then_inc(base_ready, 1)

            def normalise(n, b):
                act.wait_ge(shift_ready, layernorm_count(n, b))
                for t in tiles_of(b):
                    act.activation(xn[:, t], xs[:, t], ACT.Identity, bias=shift[:, n, t:t + 1], scale=rstd[:, n, t:t + 1]).then_inc(xn_ready, 1)

            def evacuate_xnt(fill, permuted, b):
                filled(fill[b])
                for k in range(KC):
                    last = act.copy(xn_t_view(k, b, permuted), xn_bank_view(fill[b], k, permuted))
                last.then_inc(evac["act"], 1)

            def evacuate_down(q):
                filled(F_DOWN[q])
                half, e = q // NE0, q % NE0
                for k in range(KC):
                    last = act.copy(y0_t[:, k, half * HALF:(half + 1) * HALF].rearrange("p (n e) -> p e n", e=NE0)[:, e],
                                    bank(F_DOWN[q])[:, k * TE:(k + 1) * TE])
                last.then_inc(evac["act"], 1)

            def silu_and_up0(q):
                filled(F_GATE[q])
                if q >= 2:
                    act.wait_ge(h0_ready, q - 1)
                act.activation(silu0[:, q % 2], bank(F_GATE[q])[:, 0:IC * TE], ACT.Silu).then_inc(evac["act"], 1)
                filled(F_UP[q])
                act.copy(up0[:, q % 2], bank(F_UP[q])[:, 0:IC * TE]).then_inc(evac["act"], 1)

            def exp_scores(b):
                for t in tiles_of(b):
                    act.wait_ge(ebias_ready, t + 1)
                    act.activation(work[:, t], work[:, t], ACT.Exp, bias=exp_bias[:, t:t + 1], scale=rstd[:, 2, t:t + 1],
                                   accum_out=row_sum[:, t:t + 1]).then_inc(exp_ready, 1)

            def copy_logits(b):
                filled(F_LOGIT[b])
                act.copy(logits[:, span(b)].rearrange("p h n -> p (h n)"), bank(F_LOGIT[b])[:, 0:HB * NE]).then_inc(evac["act"], 1)

            def exp_logits(b):
                act.wait_ge(l_neg_ready, b + 1)
                for t in tiles_of(b):
                    act.activation(e_val[:, t], logits[:, t], ACT.Exp, bias=l_neg[:, t:t + 1]).then_inc(e_ready, 1)

            def finish_x3(b):
                act.wait_ge(dead_ready, b + 1)
                for t in tiles_of(b):
                    act.activation(x3[:, t], xs[:, t], ACT.Identity, bias=dead_nan[:, t:t + 1]).then_inc(x3_ready, 1)

            for b in (0, 1):
                normalise(1, b)
            for b in (0, 1):
                evacuate_xnt(F_XNT, True, b)
            for q in range(NE0):
                silu_and_up0(q)
                if q:
                    evacuate_down(q - 1)
            evacuate_down(NE0 - 1)
            act.preload_act_table(ACT.Exp)
            for b in (2, 3):
                normalise(1, b)
                evacuate_xnt(F_XNT, True, b)
            exp_scores(0)
            exp_scores(1)
            act.preload_act_table(ACT.Silu)
            silu_and_up0(NE0)
            silu_and_up0(NE0 + 1)
            evacuate_down(NE0)
            normalise(3, 0)
            silu_and_up0(NE0 + 2)
            evacuate_down(NE0 + 1)
            normalise(3, 1)
            evacuate_xnt(F_XNT2, False, 0)
            evacuate_xnt(F_XNT2, False, 1)
            silu_and_up0(2 * NE0 - 1)
            copy_logits(0)
            copy_logits(1)
            evacuate_down(2 * NE0 - 2)
            evacuate_down(2 * NE0 - 1)
            act.preload_act_table(ACT.Exp)
            exp_logits(0)
            exp_logits(1)
            exp_scores(2)
            exp_scores(3)
            finish_x3(0)
            finish_x3(1)
            normalise(3, 2)
            evacuate_xnt(F_XNT2, False, 2)
            finish_x3(2)
            normalise(3, 3)
            copy_logits(2)
            evacuate_xnt(F_XNT2, False, 3)
            exp_logits(2)
            copy_logits(3)
            exp_logits(3)
            finish_x3(3)
            act.wait_ge(rw_ready, B)
            for n in range(PARTS):
                if n:
                    act.wait_ge(rest_w_ready, n)
                act.copy(w_parts[:, :, :, n], w_rest[:, n - 1] if n else rw[:]).then_inc(part_ready, 1)
            act.preload_act_table(ACT.Silu)

            def copy_lists(tile):
                act.wait_ge(list_filled, tile.j + 1)
                act.activation(w_seen[:, tile.two], psum[:, tile.two, 1:N_COLS], ACT.Copy, scale=1.0 / W_SCALE,
                               accum_out=slot_w[:, bass.ds(tile.j, 1)])
                need(act, gathered[tile.lane], tile.quad * 16)
                need(act, rows_kept, tile.j - LANES + 1)
                act.activation(gather_at[:, tile.lane:tile.lane + 1], psum[:, tile.two, 0:1], ACT.Identity,
                               bias=empty_row[:]).then_inc(list_copied, 1)

            def copy_slots_t(tile):
                need(act, gu_filled, tile.j - 1)
                act.wait_ge(xt_filled, tile.j + 1)
                act.copy(x_slots_t[:, tile.two].rearrange("p k n -> p (k n)"), psum[:, 2 + tile.two, 0:D]).then_inc(xt_copied, 1)

            def silu_gate(tile):
                act.wait_ge(gu_filled, tile.j + 1)
                need(act, h_ready, tile.j - 1)
                act.activation(silu1[:, tile.two], psum[0:I1, 4 + tile.two, 0:P], ACT.Silu).then_inc(silu1_ready, 1)

            def keep_rows(tile):
                act.wait_ge(list_copied, tile.j + 1)
                n, earlier = tile.sum()
                need(act, scattered[n], (earlier - (LANES // N_SUMS - 1)) * 16)
                act.copy(scatter_at[:, tile.lane:tile.lane + 1], gather_at[:, tile.lane:tile.lane + 1]).then_inc(rows_kept, 1)

            def weigh(tile):
                act.wait_ge(y_filled, tile.j + 1)
                act.wait_ge(list_copied, tile.j + 1)
                act.sem_inc(weighing, 1)
                act.activation(y_slots[:, tile.lane, :], psum[:, 6 + tile.two, 0:D], ACT.Copy,
                               scale=slot_w[:, bass.ds(tile.j, 1)]).then_inc(y_ready, 1)

            def slot(tile, left):
                silu_gate(tile)
                if not first(tile):
                    weigh(tile.before())
                if follows(left, 1):
                    keep_rows(tile.later(1))
                if follows(left, AHEAD):
                    copy_lists(tile.later(AHEAD))
                if follows(left, 2):
                    copy_slots_t(tile.later(2))

            for n in range(LANES):
                copy_lists(Tile(0, n))
            keep_rows(Tile(0, 0))
            copy_slots_t(Tile(0, 0))
            copy_lists(Tile(1, 0))
            copy_slots_t(Tile(0, 1))
            weigh(over_tiles(act, slot))

        @block.vector
        def _(dve):
            steps = [0]

            def link(ins):
                steps[0] += 1
                ins.then_inc(dve_step, 1)
                dve.wait_ge(dve_step, steps[0])

            def filled(i):
                dve.wait_ge(bank_filled, i + 1)

            def statistics(n, b):
                tiles, both = tiles_of(b), span(b)
                for t in tiles:
                    last = dve.bn_stats(stats[:, t], xs[:, t])
                link(last)
                for t in tiles:
                    last = dve.bn_aggr(mv[:, n, t], stats[:, t])
                link(last)
                dve.tensor_scalar(neg_mean[:, n, both], mv[:, n, both, 0], -1.0, None, ALU.mult)
                dve.tensor_scalar(var_eps[:, n, both], mv[:, n, both, 1], EPS, None, ALU.add).then_inc(var_ready, 1)

            filled(F_W)
            dve.tensor_copy(w_t[:].rearrange("p w c -> p (w c)"), bank(F_W)[0:C, 0:4 * C]).then_inc(evac["dve"], 1)
            filled(F_PROJ[1, 0])
            dve.tensor_copy(proj_t[:, 1, 0:HALF], bank(F_PROJ[1, 0])[0:C, :]).then_inc(evac["dve"], 1)
            filled(F_SIM[0])
            dve.tensor_scalar(sim[:, 0:HB, :].rearrange("p h s -> p (h s)"), bank(F_SIM[0]), SIM_SCALE, None,
                              ALU.mult).then_inc(evac["dve"], 1)

            def keep_top(b):
                emptied(dve, F_SIM[b])
                tiles = range(b * HB, (b + 1) * HB)
                for r in range(ROUNDS):
                    for t in tiles:
                        if r:
                            dve.wait_ge(rest_ready, t % HB + 1 + HB * ((ROUNDS - 1) * b + r - 1))
                        dve.max(top8[:, t, r], (work if r else sim)[:, t]).then_inc(top8_ready, 1)
                    if r < ROUNDS - 1:
                        for t in tiles:
                            dve.wait_ge(top8_ready, t % HB + 1 + HB * (ROUNDS * b + r))
                            dve.match_replace(work[:, t], top8[:, t, r], (work if r else sim)[:, t], REMOVED).then_inc(rest_ready, 1)
                dve.wait_ge(top8_ready, HB * ROUNDS * (b + 1))
                dve.wait_ge(sig_ready, b + 1)
                for t in tiles:
                    kth = top8[:, t, (TOPK - 1) // 8, (TOPK - 1) % 8:(TOPK - 1) % 8 + 1]
                    dve.scalar_tensor_tensor(out=adj[:, t], in0=sim[:, t], scalar=kth, in1=adj[:, t], op0=ALU.is_ge,
                                             op1=ALU.mult).then_inc(adj_ready, 1)

            keep_top(0)
            dve.wait_ge(ld["x"], 16)
            statistics(0, None)
            dve.wait_ge(tanh_ready, 2)
            link(dve.tensor_tensor(coef[:, 0:1], tg[:, 0:1], gam[:], ALU.mult))
            link(dve.tensor_scalar(coef[:, 1:2], coef[:, 0:1], 0.5, None, ALU.mult))
            dve.tensor_tensor(coef[:, 2:3], tg[:, 0:1], coef[:, 0:1], ALU.subtract).then_inc(coef_ready, 1)

            def mix_adjacencies(b):
                two = span(b)
                filled(F_ADJT[b])
                dve.tensor_tensor(adj[:, two].rearrange("p h s -> p (h s)"), adj[:, two].rearrange("p h s -> p (h s)"),
                                  bank(F_ADJT[b]), ALU.add).then_inc(evac["dve"], 1)
                emptied(dve, F_ADJT[b])
                dve.wait_ge(base_ready, HB * (b + 1))
                link(dve.scalar_tensor_tensor(out=xs[:, two], in0=adj[:, two], scalar=coef[:, 1:2], in1=base[:, two],
                                              op0=ALU.mult, op1=ALU.add))

            def add_layer0(b):
                filled(F_YT[b])
                dve.scalar_tensor_tensor(out=xs[:, span(b)].rearrange("p h s -> p (h s)"), in0=bank(F_YT[b]),
                                         scalar=tg[:, 2:3], in1=xs[:, span(b)].rearrange("p h s -> p (h s)"),
                                         op0=ALU.mult, op1=ALU.add).then_inc(evac["dve"], 1)
                emptied(dve, F_YT[b])

            def masked_scores(b):
                tiles = tiles_of(b)
                dve.wait_ge(rstd_ready, layernorm_count(2, b))
                for t in tiles:
                    last = dve.scalar_tensor_tensor(out=work[:, t], in0=xs[:, t], scalar=mv[:, 2, t, 0:1], in1=scores[:, t],
                                                    op0=ALU.subtract, op1=ALU.mult)
                link(last)
                for t in tiles:
                    last = dve.tensor_tensor_reduce(out=work[:, t], in0=work[:, t], in1=pen[:, t], scale=1.0, scalar=FLOOR,
                                                    op0=ALU.add, op1=ALU.max, accum_out=row_max[:, t:t + 1])
                link(last)
                for t in tiles:
                    dve.scalar_tensor_tensor(out=exp_bias[:, t:t + 1], in0=row_max[:, t:t + 1], scalar=-1.0,
                                             in1=rstd[:, 2, t:t + 1], op0=ALU.mult, op1=ALU.mult).then_inc(ebias_ready, 1)

            def add_softmax(b):
                tiles, both = tiles_of(b), span(b)
                link(dve.tensor_scalar(live[:, both], row_max[:, both], FLOOR, None, ALU.is_gt))
                link(dve.reciprocal(live[:, both], live[:, both]))
                dve.tensor_tensor(dead_nan[:, both], live[:, both], live[:, both], ALU.subtract)
                dve.wait_ge(exp_ready, tiles.stop)
                link(dve.tensor_scalar(inv_sum[:, both], row_sum[:, both], 0.5, None, ALU.max))
                link(dve.reciprocal(inv_sum[:, both], inv_sum[:, both]))
                link(dve.tensor_scalar(inv_sum[:, both], inv_sum[:, both], tg[:, 1:2], None, ALU.mult))
                for t in tiles:
                    last = dve.scalar_tensor_tensor(out=xs[:, t], in0=work[:, t], scalar=inv_sum[:, t:t + 1], in1=xs[:, t],
                                                    op0=ALU.mult, op1=ALU.add)
                link(last)
                dve.sem_inc(dead_ready, 1)

            def choose_experts(b):
                tiles, both = tiles_of(b), span(b)
                emptied(dve, F_LOGIT[b])
                for t in tiles:
                    last = dve.max(l_top[:, t], logits[:, t])
                link(last)
                dve.tensor_scalar(l_neg[:, both], l_top[:, both, 0], -1.0, None, ALU.mult).then_inc(l_neg_ready, 1)
                for t in tiles:
                    last = dve.match_replace(logits_left[:, t], l_top[:, t], logits[:, t], REMOVED)
                link(last)
                dve.tensor_scalar(chosen[:, both], logits_left[:, both], REMOVED / 2, None, ALU.is_lt).then_inc(chosen_ready, 1)

            def router_weights(b):
                tiles, both = tiles_of(b), span(b)
                dve.wait_ge(e_ready, tiles.stop)
                dve.wait_ge(chosen_ready, b + 1)
                for t in tiles:
                    last = dve.scalar_tensor_tensor(out=e_val[:, t], in0=chosen[:, t], scalar=1.0, in1=e_val[:, t], op0=ALU.mult,
                                                    op1=ALU.mult, accum_out=e_sum[:, t:t + 1])
                link(last)
                link(dve.reciprocal(e_scale[:, both], e_sum[:, both]))
                link(dve.tensor_scalar(e_scale[:, both], e_scale[:, both], tg[:, 3:4], W_SCALE, ALU.mult, ALU.mult))
                dve.tensor_tensor(rw[:, both], e_val[:, both], e_scale[:, both].rearrange("p (t a) -> p t a", a=1).to_broadcast([P, HB, NE]),
                                  ALU.mult).then_inc(rw_ready, 1)

            keep_top(1)
            for b in (0, 1):
                mix_adjacencies(b)
                statistics(1, b)
            keep_top(2)
            mix_adjacencies(2)
            statistics(1, 2)
            keep_top(3)
            mix_adjacencies(3)
            statistics(1, 3)
            for b in (0, 1):
                add_layer0(b)
                statistics(2, b)
            dve.wait_ge(pen_ready, NT)
            emptied(dve, F_SCORE[B - 1])
            masked_scores(0)
            masked_scores(1)
            for b in (0, 1):
                add_softmax(b)
                statistics(3, b)
            choose_experts(0)
            choose_experts(1)
            for b in (2, 3):
                add_layer0(b)
                statistics(2, b)
            masked_scores(2)
            masked_scores(3)
            for b in (2, 3):
                add_softmax(b)
                statistics(3, b)
            router_weights(0)
            router_weights(1)
            for b in (2, 3):
                choose_experts(b)
                router_weights(b)
            filled(F_COUNT)
            dve.tensor_scalar(n_tiles_i[:, 0], bank(F_COUNT)[:, 0:NE], float(P - 1), None, ALU.add).then_inc(evac["dve"], 1)
            emptied(dve, F_COUNT)
            link(dve.tensor_scalar(n_tiles_i[:, 1], n_tiles_i[:, 0], P.bit_length() - 1, None, ALU.arith_shift_right))
            link(dve.tensor_copy(n_tiles[:], n_tiles_i[:, 1]))
            link(dve.tensor_tensor_scan(tiles_end[:], n_tiles[:], zeros[:, 0:NE], 0.0, ALU.add, ALU.add))
            link(dve.tensor_scalar(list_scratch[:, 0], tiles_end[:], row_id[:], 0.0, ALU.is_le, ALU.add, accum_out=tile_of[:, 0:1]))
            link(dve.scalar_tensor_tensor(out=list_scratch[:, 1], in0=tiles_end[:], scalar=row_id[:], in1=n_tiles[:],
                                          op0=ALU.is_le, op1=ALU.mult, accum_out=tile_of[:, 1:2]))
            link(dve.tensor_tensor(tile_of[:, 1:2], row_id[:], tile_of[:, 1:2], ALU.subtract))
            link(dve.tensor_scalar(tile_of[:, 2:3], tile_of[:, 0:1], float(NE), float(MAX_COUNT_TILES), ALU.is_ge, ALU.mult))
            link(dve.tensor_tensor(tile_of[:, 1:2], tile_of[:, 1:2], tile_of[:, 2:3], ALU.add))
            link(dve.tensor_scalar(tile_of[:, 0:1], tile_of[:, 0:1], float(NE - 1), None, ALU.min))
            link(dve.tensor_scalar(tile_of[:, 1:2], tile_of[:, 1:2], float(P), None, ALU.mult))
            for n in range(2):
                last = dve.tensor_scalar(tile_diag[:, n], ident[:], tile_of[:, n:n + 1], None, ALU.mult)
            last.then_inc(diag_ready, 1)
            filled(F_RANK)
            link(dve.scalar_tensor_tensor(out=rank[:].rearrange("p t e -> p (t e)"), in0=bank(F_RANK), scalar=1.0,
                                          in1=chosen[:].rearrange("p t e -> p (t e)"), op0=ALU.add, op1=ALU.mult))
            dve.tensor_scalar(rank[:], rank[:], -1.0, None, ALU.add).then_inc(evac["dve"], 1)
            link(dve.tensor_scalar(n_tiles_i[0:1, 0, 0:1], tiles_end[0:1, NE - 1:NE], float(LANES - 1), None, ALU.add))
            link(dve.tensor_scalar(n_tiles_i[0:1, 1, 0:1], n_tiles_i[0:1, 0, 0:1], LANES.bit_length() - 1, None, ALU.arith_shift_right))
            link(dve.tensor_scalar(n_quads[0:1, 0:1], n_tiles_i[0:1, 1, 0:1], float(FIRST_QUADS + LAST_QUADS), None, ALU.subtract))
            filled(F_TILES)
            dve.tensor_copy(first_rank[:], bank(F_TILES)[:, P:2 * P])
            dve.tensor_copy(expert_of[:], bank(F_TILES)[0:1, 0:P]).then_inc(evac["dve"], 1)
            emptied(dve, F_TILES)
            dve.sem_inc(lists_ready, 1)

            def load_expert(tile):
                return dve.value_load(expert_of[0:1, bass.ds(tile.j, 1)], min_val=0, max_val=NE - 1)

            def prepare(tile, e):
                need(dve, list_filled, tile.j - 1)
                two = tile.two
                dve.tensor_tensor(local[:, two], rank[:, :, bass.ds(e, 1)].rearrange("p t a -> p (t a)"),
                                  first_rank[:, bass.ds(tile.j, 1)].to_broadcast([P, NT]), ALU.subtract).then_inc(local_ready, 1)
                dve.wait_ge(local_ready, tile.j + 1)
                dve.tensor_tensor(cols[:, two, :, 0], token_id[:], local[:, two], ALU.subtract)
                if first(tile):
                    dve.wait_ge(part_ready, PARTS)
                dve.tensor_copy(cols[:, two, :, 1:N_COLS], w_parts[:, :, bass.ds(e, 1), :].rearrange("p t a n -> p t (a n)"))
                dve.tensor_tensor(one_hot[:, two], slot_id[:], local[:, two:two + 1].to_broadcast([P, P, NT]),
                                  ALU.is_equal).then_inc(cols_ready, 1)

            def up_times_silu1(tile):
                dve.wait_ge(silu1_ready, tile.j + 1)
                need(dve, y_filled, tile.j - 1)
                dve.tensor_tensor(h1_t[:, tile.two], silu1[:, tile.two], psum[0:I1, 4 + tile.two, P:2 * P], ALU.mult).then_inc(h_ready, 1)

            def slot(tile, left):
                e = load_expert(tile.later(AHEAD)) if follows(left, AHEAD) else None
                if not first(tile):
                    up_times_silu1(tile.before())
                if follows(left, AHEAD):
                    prepare(tile.later(AHEAD), e)

            for n in range(AHEAD):
                prepare(Tile(0, 0).later(n), load_expert(Tile(0, 0).later(n)))
            up_times_silu1(over_tiles(dve, slot))
            for c in range(B):
                tiles = slice(c * HB, (c + 1) * HB)
                dve.wait_ge(sums_loaded[c], 16 * N_SUMS)
                dve.tensor_tensor(xs[:, tiles], base[:, tiles], adj[:, tiles], ALU.add).then_inc(out_ready, 1)



_INS = ["x", "ctx_512", "mask_SxS2_bk1", "mask_BxS2_bf0", "g_xattn", "g_ffn", "L0_xattn_Wq", "L0_xattn_Wk",
        "L0_xattn_gamma_raw", "L0_ffn_gate_up_proj", "L0_ffn_down_proj", "L1_xattn_Wq", "L1_xattn_bq", "L1_xattn_Wk",
        "L1_xattn_bk", "L1_ffn_gate_w", "L1_ffn_w_gate", "L1_ffn_w_up", "L1_ffn_w_down"]


def kernel(**inputs):
    import numpy as _np
    import concourse.bacc as _bacc
    from concourse import mybir as _mybir
    from concourse.bass_utils import run_bass_kernel_spmd as _run

    nc = _bacc.Bacc("TRN2", target_bir_lowering=False, num_devices=1)
    arrays, args = {}, []
    for name in _INS:
        a = _np.ascontiguousarray(inputs[name])
        if a.ndim == 0:
            a = a.reshape(1, 1)
        arrays[f"in_{name}"] = a
        args.append(nc.dram_tensor(f"in_{name}", a.shape, _mybir.dt.from_np(a.dtype), kind="ExternalInput").ap())
    x = arrays["in_x"]
    out = nc.dram_tensor("out_0", x.shape, _mybir.dt.from_np(x.dtype), kind="ExternalOutput").ap()
    gated_layers_kernel(nc, *args, out)
    r = _run(nc, [arrays], core_ids=[0])
    return r.results[0]["out_0"]
```
